# Optimizing a Trainium2 kernel written in Bass

```python
import numpy as np
import jax
import jax.numpy as jnp

def _softmax(x, axis=-1):
    return jax.nn.softmax(x, axis=axis)

def _gelu(x):
    return jax.nn.gelu(x, approximate=True)

def _silu(x):
    return jax.nn.silu(x)

def _sigmoid(x):
    return jax.nn.sigmoid(x)

def _layernorm(x, axis=-1, eps=1e-05):
    m = jnp.mean(x, axis=axis, keepdims=True)
    v = jnp.var(x, axis=axis, keepdims=True)
    return (x - m) / jnp.sqrt(v + eps)

def _scatter_add(tgt, idx, src, axis=0):
    return tgt.at[idx].add(src)

def _segment_sum(src, seg, n):
    return jax.ops.segment_sum(src, seg, n)
kernel_name = 'mk_seq_preln_d1_jaxref_r8_cb7c18'

def setup_inputs(seed: int=0):
    np.random.seed(seed)
    _w = jnp.asarray

    def _L0_attn_setup():
        import jax, jax.numpy as jnp
        import numpy as np
        DIM = 128
        HEADS = 16
        DIM_HEAD = DIM // HEADS
        LATENT = DIM // 4
        SCALE = DIM_HEAD ** (-0.5)
        key = jax.random.key(seed)
        ks = jax.random.split(key, 8)
        B, S = (2, 256)
        init = lambda k, shape, fan_in: jax.random.normal(k, shape, jnp.float32) * fan_in ** (-0.5)
        return {'x': jax.random.normal(ks[0], (B, S, DIM), jnp.float32), 'Wq': init(ks[1], (DIM, DIM), DIM), 'bq': jnp.zeros((DIM,), jnp.float32), 'Wl': init(ks[2], (DIM, LATENT), DIM), 'bl': jnp.zeros((LATENT,), jnp.float32), 'Wk': init(ks[3], (LATENT, DIM), LATENT), 'bk': jnp.zeros((DIM,), jnp.float32), 'Wv': init(ks[4], (LATENT, DIM), LATENT), 'bv': jnp.zeros((DIM,), jnp.float32), 'Wo': init(ks[5], (DIM, DIM), DIM), 'bo': jnp.zeros((DIM,), jnp.float32)}
    _L0_attn_in = _L0_attn_setup()

    def _L0_ffn_setup():
        import jax, jax.numpy as jnp
        import numpy as np
        D_MODEL = 128
        N_EXPERTS = 8
        TOP_K = 2
        FFN_HIDDEN = 4 * D_MODEL
        key = jax.random.key(seed)
        ks = jax.random.split(key, 6)

        def xavier(k, shape):
            fan_in, fan_out = (shape[-2], shape[-1])
            lim = jnp.sqrt(6.0 / (fan_in + fan_out))
            return jax.random.uniform(k, shape, jnp.float32, -lim, lim)
        x = jax.random.normal(ks[0], (4, 256, D_MODEL), jnp.float32)
        w_gate = xavier(ks[1], (N_EXPERTS, D_MODEL))
        W1 = xavier(ks[2], (N_EXPERTS, D_MODEL, FFN_HIDDEN))
        b1 = jnp.zeros((N_EXPERTS, FFN_HIDDEN), jnp.float32)
        W2 = xavier(ks[3], (N_EXPERTS, FFN_HIDDEN, D_MODEL))
        b2 = jnp.zeros((N_EXPERTS, D_MODEL), jnp.float32)
        return {'x': x, 'w_gate': w_gate, 'W1': W1, 'b1': b1, 'W2': W2, 'b2': b2}
    _L0_ffn_in = _L0_ffn_setup()
    _d = {'L0_attn_x': _L0_attn_in['x'], 'L0_attn_Wq': _L0_attn_in['Wq'], 'L0_attn_bq': _L0_attn_in['bq'], 'L0_attn_Wl': _L0_attn_in['Wl'], 'L0_attn_bl': _L0_attn_in['bl'], 'L0_attn_Wk': _L0_attn_in['Wk'], 'L0_attn_bk': _L0_attn_in['bk'], 'L0_attn_Wv': _L0_attn_in['Wv'], 'L0_attn_bv': _L0_attn_in['bv'], 'L0_attn_Wo': _L0_attn_in['Wo'], 'L0_attn_bo': _L0_attn_in['bo'], 'L0_ffn_w_gate': _L0_ffn_in['w_gate'], 'L0_ffn_W1': _L0_ffn_in['W1'], 'L0_ffn_b1': _L0_ffn_in['b1'], 'L0_ffn_W2': _L0_ffn_in['W2'], 'L0_ffn_b2': _L0_ffn_in['b2']}
    _x0 = _d['L0_attn_x']
    _d['L0_attn_x'] = jax.random.normal(jax.random.fold_in(jax.random.key(seed), 1), (8, 512, 128), dtype=_x0.dtype)
    del _x0
    return _d

def reference(L0_attn_x, L0_attn_Wq, L0_attn_bq, L0_attn_Wl, L0_attn_bl, L0_attn_Wk, L0_attn_bk, L0_attn_Wv, L0_attn_bv, L0_attn_Wo, L0_attn_bo, L0_ffn_w_gate, L0_ffn_W1, L0_ffn_b1, L0_ffn_W2, L0_ffn_b2):

    def _L0_attn_ref(x, Wq, bq, Wl, bl, Wk, bk, Wv, bv, Wo, bo):
        import jax, jax.numpy as jnp
        import numpy as np
        DIM = 128
        HEADS = 16
        DIM_HEAD = DIM // HEADS
        LATENT = DIM // 4
        SCALE = DIM_HEAD ** (-0.5)
        B, S, D = x.shape
        H, Dh = (HEADS, DIM_HEAD)
        q = (x @ Wq + bq).reshape(B, S, H, Dh)
        latent = x @ Wl + bl
        k = (latent @ Wk + bk).reshape(B, S, H, Dh)
        v = (latent @ Wv + bv).reshape(B, S, H, Dh)
        scores = jnp.einsum('bihd,bjhd->bhij', q, k) * SCALE
        attn = jax.nn.softmax(scores, axis=-1)
        out = jnp.einsum('bhij,bjhd->bihd', attn, v).reshape(B, S, D)
        out = out @ Wo + bo
        return out

    def _L0_ffn_ref(x, w_gate, W1, b1, W2, b2):
        import jax, jax.numpy as jnp
        import numpy as np
        D_MODEL = 128
        N_EXPERTS = 8
        TOP_K = 2
        FFN_HIDDEN = 4 * D_MODEL
        B, S, D = x.shape
        flat_x = x.reshape(-1, D)
        gate = jax.nn.softmax(flat_x @ w_gate.T, axis=-1)
        topk_scores, topk_idx = jax.lax.top_k(gate, TOP_K)
        cw = (jax.nn.one_hot(topk_idx, N_EXPERTS, dtype=flat_x.dtype) * topk_scores[..., None]).sum(axis=1)
        h = jax.nn.gelu(jnp.einsum('td,edh->teh', flat_x, W1) + b1, approximate=False)
        y = jnp.einsum('teh,ehd->ted', h, W2) + b2
        out = jnp.einsum('ted,te->td', y, cw)
        return out.reshape(B, S, D)
    x = L0_attn_x
    x = x + _L0_attn_ref(_layernorm(x, axis=-1), L0_attn_Wq, L0_attn_bq, L0_attn_Wl, L0_attn_bl, L0_attn_Wk, L0_attn_bk, L0_attn_Wv, L0_attn_bv, L0_attn_Wo, L0_attn_bo)
    x = x + _L0_ffn_ref(_layernorm(x, axis=-1), L0_ffn_w_gate, L0_ffn_W1, L0_ffn_b1, L0_ffn_W2, L0_ffn_b2)
    return x

_drawn_inputs = setup_inputs


def setup_inputs(seed=0):
    import zlib

    import numpy as np

    out = dict(_drawn_inputs(seed))
    spreads = {'L0_attn_bq': (0.0, 0.34),
     'L0_attn_bl': (0.0, 0.1),
     'L0_attn_bk': (0.0, 0.8),
     'L0_attn_bv': (0.0, 0.1),
     'L0_attn_bo': (0.0, 0.1),
     'L0_ffn_b1': (0.0, 0.1),
     'L0_ffn_b2': (0.0, 0.1)}
    factors = {}
    for name, (base, spread) in spreads.items():
        noise = np.random.default_rng([zlib.crc32(name.encode()), seed]).standard_normal(out[name].shape)
        drawn = base * np.exp(spread * noise) if base else spread * noise
        out[name] = jnp.asarray(drawn.astype(out[name].dtype))
    for name, factor in factors.items():
        out[name] = (out[name] * factor).astype(out[name].dtype)
    return out
```

```python
from contextlib import ExitStack, nullcontext

import concourse.bass as bass
from concourse import mybir

ALU = mybir.AluOpType
ACT = mybir.ActivationFunctionType
F32 = mybir.dt.float32
F32R = mybir.dt.float32r
BF16 = mybir.dt.bfloat16
AX_X = mybir.AxisListType.X

P = 128
TWO_ONES = 0x3F803F80
LN_EPS = 1e-5

UNITS = 16
AHEAD = 8
GROUP = 4
ROWS = 48
MAX_ROW = 96

STEPS = [
    (0, 1, "max_rows", 0, 1), (1, 1, "heads", -1, 3), (2, 1, "heads_t", -1, 0), (3, 1, "project", -1, 0),
    (4, 1, "max_rows", 0, 2), (5, 0, "value", 1, 0), (5, 1, "normed", 2, 0), (6, 0, "heads", 0, 0),
    (6, 1, "query", 2, 0), (7, 0, "normed2", -1, 0), (7, 1, "latent", 2, 0), (8, 0, "gate", -1, 0),
    (8, 1, "max_rows", 0, 3), (9, 0, "key", 2, 0), (9, 1, "heads", 0, 1), (12, 1, "max_rows", 1, 0),
    (13, 0, "gate_t", -1, 0), (13, 1, "heads", 0, 2),
]
PER_BATCH = {"max_rows": 4, "heads": 4}
READS = {"max_rows": 2, "query": 2, "key": 2, "normed2": 2}
STEP_NAMES = sorted({s[2] for s in STEPS})


class Signal:

    def __init__(self, sem, per_batch, by=1):
        self.sem, self.per_batch, self.by = sem, per_batch, by

    def at(self, b, k):
        return b * (self.per_batch * self.by) + k * self.by

    def due(self, b, k):
        return not isinstance(b, int) or self.at(b, k) > 0


def block_attention_moe(nc, x, wq, bq, wl, bl, wk, bk, wv, bv, wo, bo, w_gate_t, w1, b1_t, w2, b2_t, out):
    NB, S, D = x.shape
    NE, _, F = w1.shape
    LAT = wl.shape[1]
    H, DH = 16, 8
    assert H * DH == D == P and S == 4 * P
    C = S // P
    HC = F // P
    SCALE = float(DH) ** -0.5
    NT = UNITS * GROUP
    HU = NE * HC
    LAG = 3

    ctx = ExitStack()
    with ctx:
        def sb(name, shape, dt=F32):
            return ctx.enter_context(nc.sbuf_tensor(name, shape, dt))

        def sem(name):
            return ctx.enter_context(nc.semaphore(name))

        def signal(name, per_batch, by=1):
            return Signal(sem(name), per_batch, by)

        psum = ctx.enter_context(nc.psum_tensor("psum", [P, 8, S], F32))
        SCORE, MAXIMA, PV, SHARED = (0, 1, 2), (3, 4, 5), 6, 7
        HIDDEN, EXPERT_OUT = (0, 1, 2, 3), (4, 5)

        X = sb("X", [P, NB * S])
        x2_hi = sb("x2_hi", [P, NB * S], F32R)
        x2_lo = sb("x2_lo", [P, NB * S], F32R)
        ident = sb("ident", [P, P])
        wq_sb, wo_sb = sb("wq_sb", [P, D]), sb("wo_sb", [P, D])
        wl_sb, wk_sb, wv_sb = sb("wl_sb", [P, LAT]), sb("wk_sb", [LAT, D]), sb("wv_sb", [LAT, D])
        wg_sb, b1_sb, b2_sb = sb("wg_sb", [P, NE]), sb("b1_sb", [P, HU]), sb("b2_sb", [P, NE])
        bq_sb, bk_sb, bl_sb = sb("bq_sb", [P, 1]), sb("bk_sb", [P, 1]), sb("bl_sb", [LAT, 1])
        bv_row, bo_row = sb("bv_row", [P, D]), sb("bo_row", [P, D])
        earlier, later = sb("earlier", [P, NE, NE]), sb("later", [P, NE, NE])
        minus_half, eps = sb("minus_half", [P, C]), sb("eps", [P, C])

        stack_base = -(-nc.sbuf_base // 32) * 32
        Q_stack = [sb(f"Q_stack{i}", [P, H, S], BF16) for i in range(2)]
        K_stack = [sb(f"K_stack{i}", [P, H, S], BF16) for i in range(2)]
        probs = sb("probs", [P, 2, GROUP, S])
        values = sb("values", [P, 2, C, H, 32])
        pv_sb = sb("pv_sb", [P, 2, S])
        xn, xn2 = sb("xn", [P, C, D]), sb("xn2", [P, C, D])
        xn_t, lat_t = sb("xn_t", [P, S]), sb("lat_t", [LAT, S])
        q_sb, k_sb, rest = sb("q_sb", [P, S]), sb("k_sb", [P, S]), sb("rest", [P, S])
        q_parts, k_parts = sb("q_parts", [P, 3, S], BF16), sb("k_parts", [P, 3, S], BF16)
        heads, heads_t, x2_f = sb("heads", [P, C, H, DH]), sb("heads_t", [P, S]), sb("x2_f", [P, S])
        inv_sum = sb("inv_sum", [P, C, GROUP])
        stats, mv, rstd = sb("stats", [P, C, 6]), sb("mv", [P, C, 2]), sb("rstd", [P, C])
        stats2, mv2, rstd2 = sb("stats2", [P, C, 6]), sb("mv2", [P, C, 2]), sb("rstd2", [P, C])
        neg_max = sb("neg_max", [P, 2, 16])
        max_sb, max_rest = sb("max_sb", [16, P]), sb("max_rest", [16, P])
        max_parts = sb("max_parts", [16, 3, P], BF16)
        g_max, g_sum, g_inv = sb("g_max", [P, C]), sb("g_sum", [P, C]), sb("g_inv", [P, C])
        g_z, g_e, g_p = sb("g_z", [P, C, NE]), sb("g_e", [P, C, NE]), sb("g_p", [P, C, NE])
        g_ge, g_gt = sb("g_ge", [P, C, NE, NE]), sb("g_gt", [P, C, NE, NE])
        g_rank, cw, cw_t = sb("g_rank", [P, C, NE]), sb("cw", [P, C, NE]), sb("cw_t", [NE, S])

        size = H * S * 2
        h_sb = sb("h_sb", [P, 4, S])
        scaled, acc, total = sb("scaled", [P, 2, S]), sb("acc", [P, S]), sb("total", [P, C, P])
        result = sb("result", [P, C, D])
        w_raw = sb("w_raw", [P, 2, F])

        def over(name, shape, dt, offset):
            return nc.alloc_sbuf_tensor_at(name, shape, dt, offset=offset)

        w1_hi = over("w1_hi", [P, NE, F], F32R, stack_base)
        w2_hi = over("w2_hi", [P, NE, HC, D], F32R, stack_base + size)
        w1_lo = over("w1_lo", [P, NE, F], F32R, stack_base + 2 * size)
        w2_lo = over("w2_lo", [P, NE, HC, D], F32R, stack_base + 3 * size)
        h_hi = over("h_hi", [P, 4, S], F32R, stack_base + 4 * size)
        h_lo = over("h_lo", [P, 4, S], F32R, stack_base + 4 * size + 4 * S * 4)
        cw_row = over("cw_row", [P, NE, S], F32, stack_base + 4 * size + 8 * S * 4)

        q_dram = nc.dram_tensor("q_dram", [2, H, ROWS, S], BF16).ap()
        k_dram = nc.dram_tensor("k_dram", [2, H, ROWS, S], BF16).ap()
        cw_dram = nc.dram_tensor("cw_dram", [NB * NE, S], F32).ap()

        x_loaded = [sem(f"x_loaded{i}") for i in range(3)]
        small_loaded = sem("small_loaded")
        consts_made = sem("consts_made")
        stack_cleared, rows_set = sem("stack_cleared"), sem("rows_set")
        ones_made = sem("ones_made")
        full = {n: signal(f"{n}_in_psum", PER_BATCH.get(n, 1)) for n in STEP_NAMES}
        taken = {n: signal(f"{n}_taken", READS.get(n, 1) * PER_BATCH.get(n, 1)) for n in STEP_NAMES}
        score_full, exp_done = signal("score_full", NT), signal("exp_done", NT)
        max_full, max_read = signal("max_full", NT), signal("max_read", NT)
        pv_done, pv_copied = signal("pv_done", UNITS), signal("pv_copied", GROUP)
        stats_made, mv_made = signal("stats_made", C), signal("mv_made", C)
        var_made, rstd_made, xn_made = signal("var_made", 1), signal("rstd_made", 1), signal("xn_made", C)
        stats2_made, mv2_made = signal("stats2_made", C), signal("mv2_made", C)
        var2_made, rstd2_made, xn2_made = signal("var2_made", 1), signal("rstd2_made", 1), signal("xn2_made", C)
        bo_added, residual_made = signal("bo_added", 1), signal("residual_made", 1)
        q_split, k_split, m_split = signal("q_split", 3), signal("k_split", 3), signal("m_split", 12)
        q_stored, k_stored = signal("q_stored", 6, 16), signal("k_stored", 6, 16)
        stacked = [signal(f"stacked{g}", 2, 16) for g in range(4)]
        m_stored = signal("m_stored", 12, 16)
        inv_made = signal("inv_made", 4)
        x2_split = signal("x2_split", 1)
        g_max_made, g_exp_done, g_sum_made = signal("g_max_made", 1), signal("g_exp_done", 1), signal("g_sum_made", 1)
        g_inv_made, g_p_made, g_compared = signal("g_inv_made", 1), signal("g_p_made", 1), signal("g_compared", 2)
        g_masked, g_counted, g_ranked = signal("g_masked", 2), signal("g_counted", 1), signal("g_ranked", 1)
        cw_made, cw_stored = signal("cw_made", 1), signal("cw_stored", 1, 16)
        w_loaded = [sem(f"w_loaded{i}") for i in range(2)]
        w_hi_made, w_split = sem("w_hi_made"), sem("w_split")
        hidden_full, gelu_done = signal("hidden_full", HU), signal("gelu_done", HU)
        h_hi_made, h_lo_made = signal("h_hi_made", HU), signal("h_lo_made", HU)
        second_done = signal("second_done", HU)
        scaled_made, added = signal("scaled_made", NE), signal("added", NE - 1)
        cw_loaded = [signal(f"cw_loaded{e}", 1, 16) for e in range(NE)]
        total_in_psum, result_made = signal("total_in_psum", 1), signal("result_made", 1)
        result_stored = signal("result_stored", 1, 16)

        block = ctx.enter_context(nc.Block())

        def exists(b):
            return not isinstance(b, int) or 0 <= b < NB

        def run_slots(eng, slot, after_first=lambda: None):
            slot(-2, 0)
            after_first()
            for b in (-1, 0, 1):
                slot(b, b % 2)
            with eng.Fori(2, 5, 2) as b:
                slot(b, 0)
                slot(b + 1, 1)
            for b in range(6, NB + 1):
                slot(b, b % 2)

        def run_experts(eng, batch):
            batch(0, False, True)
            batch(1, True, True)
            with eng.Fori(2, NB - 1) as t:
                batch(t, True, True)
            batch(NB - 1, True, True)
            batch(NB, True, False)

        def steps_at(b, u, half):
            return [(n, b + db, g) for v, w, n, db, g in STEPS if (v, w) == (u, half) and exists(b + db)]

        def maxima_at(b, u):
            return (b, u + AHEAD) if u < UNITS - AHEAD else (b + 1, u + AHEAD - UNITS)

        def bank_of(banks, n, parity):
            return banks[(n + parity) % len(banks)]

        def bank_freed(banks, n, b, parity):
            if n >= len(banks):
                return b, n - len(banks) + 1
            before = max(m for m in range(NT) if bank_of(banks, m, 1 - parity) == bank_of(banks, n, parity))
            return b - 1, before + 1

        def wait_x(eng, b):
            eng.wait_ge(x_loaded[min(b, 2)] if isinstance(b, int) else x_loaded[2],
                        16 if isinstance(b, int) and b < 2 else 16 * (NB - 2))

        def tokens(b, c=0, n=1):
            return bass.ds(b * S + c * P, n * P)

        @block.sync
        def _(sp):
            def load_x(b):
                sp.dma_start(X[:, tokens(b, 0, C)].rearrange("p (c d) -> p c d", c=C),
                             x[b].rearrange("(c p) d -> p c d", p=P)).then_inc(x_loaded[min(b, 2)], 16)

            load_x(0)
            for dst, src in ((wq_sb, wq), (wl_sb, wl), (wk_sb, wk), (wv_sb, wv), (wo_sb, wo), (wg_sb, w_gate_t),
                             (b1_sb, b1_t), (b2_sb, b2_t),
                             (bq_sb, bq.rearrange("(p a) -> p a", a=1)), (bk_sb, bk.rearrange("(p a) -> p a", a=1)),
                             (bl_sb, bl.rearrange("(p a) -> p a", a=1)),
                             (bv_row, bv.partition_broadcast(P)), (bo_row, bo.partition_broadcast(P))):
                sp.dma_start(dst[:], src).then_inc(small_loaded, 16)
            for b in range(1, NB):
                load_x(b)

            def stack(b, parity, g):
                hs = slice(GROUP * g, GROUP * (g + 1))
                for stk, dram in ((Q_stack, q_dram), (K_stack, k_dram)):
                    sp.dma_start(stk[parity][0:ROWS, hs, :],
                                 dram[parity, hs].rearrange("h r n -> r h n")).then_inc(stacked[g].sem, 16)

            def store_parts(b, parity):
                for parts, order, dram, ready, stored in ((q_parts, (0, 0, 0, 1, 1, 2), q_dram, q_split, q_stored),
                                                          (k_parts, (0, 1, 2, 0, 1, 0), k_dram, k_split, k_stored)):
                    sp.wait_ge(ready.sem, ready.at(b, 3))
                    for r, part in enumerate(order):
                        sp.dma_start(dram[parity, :, r * DH:(r + 1) * DH, :], parts[:, part, :]).then_inc(stored.sem, 16)
                sp.wait_ge(q_stored.sem, q_stored.at(b, 6))
                sp.wait_ge(k_stored.sem, k_stored.at(b, 6))

            def max_rows(b, parity, g):
                sp.wait_ge(m_split.sem, m_split.at(b, 3 * (g + 1)))
                for part in range(3):
                    sp.dma_start(Q_stack[parity][MAX_ROW + part:MAX_ROW + part + 1, GROUP * g:GROUP * (g + 1), :],
                                 max_parts[:, part, :]).then_inc(m_stored.sem, 16)

            def slot(b, parity):
                if exists(b + 1):
                    if score_full.due(b - 1, NT):
                        sp.wait_ge(score_full.sem, score_full.at(b - 1, NT))
                    stack(b + 1, 1 - parity, 3)
                for u in range(UNITS):
                    if u == 12:
                        if exists(b + 2):
                            store_parts(b + 2, parity)
                            if isinstance(b, int) and b == -2:
                                sp.wait_ge(stack_cleared, 2)
                                sp.wait_ge(rows_set, 4)
                            for g in (0, 1, 2):
                                if exists(b):
                                    sp.wait_ge(score_full.sem, score_full.at(b, 16 * (g + 1)))
                                stack(b + 2, parity, g)
                    for half in range(2):
                        for name, bb, g in steps_at(b, u, half):
                            if name == "max_rows":
                                max_rows(bb, parity if u < 12 else 1 - parity, g)
                            if name == "gate_t":
                                sp.wait_ge(taken["gate_t"].sem, taken["gate_t"].at(bb, 1))
                                sp.dma_start(cw_dram[bass.ds(bb * NE, NE), :], cw_t[:]).then_inc(cw_stored.sem, 16)

            run_slots(sp, slot)

            sp.wait_ge(pv_done.sem, pv_done.at(NB - 1, UNITS))
            sp.wait_ge(cw_stored.sem, cw_stored.at(NB - 1, 1))
            for e in range(NE):
                sp.dma_start(cw_row[:, e, :], cw_dram[e].partition_broadcast(P)).then_inc(cw_loaded[e].sem, 16)
            def batch(t, before, now):
                for s in range(UNITS * 2 if now else 8):
                    if s == 2 and before and now:
                        if scaled_made.due(t - 1, NE):
                            sp.wait_ge(scaled_made.sem, scaled_made.at(t - 1, NE))
                        sp.dma_start(cw_row[:, NE - 1, :],
                                     cw_dram[t * NE + (NE - 1)].partition_broadcast(P)
                                     if isinstance(t, int) else
                                     cw_dram[bass.ds(t * NE + (NE - 1), 1), :].rearrange("a n -> (a n)").partition_broadcast(P)
                                     ).then_inc(cw_loaded[NE - 1].sem, 16)
                    if s == 7 and before:
                        if result_made.due(t - 1, 1):
                            sp.wait_ge(result_made.sem, result_made.at(t - 1, 1))
                        sp.dma_start(out[bass.ds(t - 1, 1)].rearrange("a (c p) d -> p (a c) d", p=P),
                                     result[:]).then_inc(result_stored.sem, 16)
                    if now and s >= 6 and (s - 6) % 4 == 0 and not (isinstance(t, int) and t + 1 >= NB):
                        e = (s - 6) // 4
                        sp.wait_ge(scaled_made.sem, scaled_made.at(t, e + 1))
                        if isinstance(t, int):
                            src = cw_dram[(t + 1) * NE + e]
                        else:
                            src = cw_dram[bass.ds((t + 1) * NE + e, 1), :].rearrange("a n -> (a n)")
                        sp.dma_start(cw_row[:, e, :], src.partition_broadcast(P)).then_inc(cw_loaded[e].sem, 16)

            run_experts(sp, batch)
            sp.wait_ge(result_stored.sem, result_stored.at(NB - 1, 1))

        @block.gpsimd
        def _(pool):
            pool.memset(ident[:], 0.0).then_inc(consts_made, 1)
            pool.memset(earlier[:], 1.0).then_inc(consts_made, 1)
            pool.memset(later[:], 1.0).then_inc(consts_made, 1)
            pool.memset(minus_half[:], -0.5).then_inc(consts_made, 1)
            pool.memset(eps[:], LN_EPS).then_inc(consts_made, 1)
            pool.wait_ge(consts_made, 5)
            pool.affine_select(out=ident[:], in_=ident[:], compare_op=ALU.not_equal, fill=1.0, base=0,
                               pattern=[[-1, P]], channel_multiplier=1).then_inc(consts_made, 1)
            pool.affine_select(out=earlier[:], in_=earlier[:], compare_op=ALU.is_gt, fill=0.0, base=0,
                               pattern=[[1, NE], [-1, NE]], channel_multiplier=0).then_inc(consts_made, 1)
            pool.affine_select(out=later[:], in_=later[:], compare_op=ALU.is_gt, fill=0.0, base=0,
                               pattern=[[-1, NE], [1, NE]], channel_multiplier=0).then_inc(consts_made, 1)
            pool.wait_ge(consts_made, 8)

            def inverse_std(b, mv_, rstd_, mvm, var, rs):
                pool.wait_ge(mvm.sem, mvm.at(b, C))
                pool.tensor_tensor(rstd_[:], mv_[:, :, 1], eps[:], ALU.add).then_inc(var.sem, 1)
                pool.wait_ge(var.sem, var.at(b, 1))
                pool.tensor_tensor(rstd_[:], rstd_[:], minus_half[:], ALU.pow).then_inc(rs.sem, 1)

            def split(b, src, parts, ready, sig):
                pool.wait_ge(ready.sem, ready.at(b, 2))
                pool.tensor_tensor(rest[:], src[:], parts[:, 0, :], ALU.subtract).then_inc(sig.sem, 1)
                if sig is q_split:
                    add_bo(b)
                pool.tensor_tensor(parts[:, 1, :], src[:], parts[:, 0, :], ALU.subtract).then_inc(sig.sem, 1)
                pool.wait_ge(sig.sem, sig.at(b, 2))
                pool.tensor_tensor(parts[:, 2, :], rest[:], parts[:, 1, :], ALU.subtract).then_inc(sig.sem, 1)

            def split_max(b, g):
                pool.wait_ge(taken["max_rows"].sem, taken["max_rows"].at(b, 2 * (g + 1)))
                pool.tensor_tensor(max_rest[:], max_sb[:], max_parts[:, 0, :], ALU.subtract).then_inc(m_split.sem, 1)
                pool.tensor_tensor(max_parts[:, 1, :], max_sb[:], max_parts[:, 0, :], ALU.subtract).then_inc(m_split.sem, 1)
                if m_split.due(b, 3 * g + 2):
                    pool.wait_ge(m_split.sem, m_split.at(b, 3 * g + 2))
                pool.tensor_tensor(max_parts[:, 2, :], max_rest[:], max_parts[:, 1, :], ALU.subtract).then_inc(m_split.sem, 1)

            def add_bo(b):
                res = X[:, tokens(b, 0, C)].rearrange("p (c d) -> p c d", c=C)
                pool.tensor_tensor(res, res, bo_row[:].rearrange("p (a d) -> p a d", a=1).to_broadcast([P, C, D]),
                                   ALU.add).then_inc(bo_added.sem, 1)

            def gate_masks(b):
                pool.wait_ge(g_compared.sem, g_compared.at(b, 2))
                pool.tensor_tensor(g_ge[:], g_ge[:], earlier_b, ALU.mult).then_inc(g_masked.sem, 1)
                pool.tensor_tensor(g_gt[:], g_gt[:], later_b, ALU.mult).then_inc(g_masked.sem, 1)
                pool.wait_ge(g_masked.sem, g_masked.at(b, 2))
                pool.tensor_tensor(g_ge[:], g_ge[:], g_gt[:], ALU.add).then_inc(g_counted.sem, 1)

            earlier_b = earlier[:].rearrange("p (a e) f -> p a e f", a=1).to_broadcast([P, C, NE, NE])
            later_b = later[:].rearrange("p (a e) f -> p a e f", a=1).to_broadcast([P, C, NE, NE])

            def slot(b, parity):
                for u in range(UNITS):
                    for half in range(2):
                        if (u, half) == (3, 0) and exists(b + 2):
                            inverse_std(b + 2, mv, rstd, mv_made, var_made, rstd_made)
                        if (u, half) == (5, 0) and exists(b - 1):
                            inverse_std(b - 1, mv2, rstd2, mv2_made, var2_made, rstd2_made)
                        if (u, half) == (9, 1) and exists(b - 1):
                            gate_masks(b - 1)
                        for name, bb, g in steps_at(b, u, half):
                            if name == "max_rows":
                                split_max(bb, g)
                            if name == "query":
                                pool.wait_ge(xn_made.sem, xn_made.at(bb, C))
                                if k_split.due(bb - 1, 3):
                                    pool.wait_ge(k_split.sem, k_split.at(bb - 1, 3))
                                split(bb, q_sb, q_parts, taken["query"], q_split)
                            if name == "key":
                                pool.wait_ge(q_split.sem, q_split.at(bb, 3))
                                split(bb, k_sb, k_parts, taken["key"], k_split)
                        if (u % 2, half) == (0, 1) and isinstance(b, int) and b == NB - 1:
                            if u == 0:
                                pool.wait_ge(score_full.sem, score_full.at(NB - 2, NT))
                            split_w(u // 2)
                        if half == 1 and u in (0, 2, 5, 6, 8, 10, 11, 12) and isinstance(b, int) and b == NB:
                            if u == 0:
                                pool.wait_ge(score_full.sem, score_full.at(NB - 1, NT))
                            split_w(NE + (0, 2, 5, 6, 8, 10, 11, 12).index(u))

            def load_w(i):
                e = i % NE
                if i < NE:
                    dst, src = w_raw[:, i % 2, :], w1[e]
                else:
                    dst, src = w_raw[:, i % 2, :].rearrange("p (c d) -> p c d", c=HC), w2[e].rearrange("(c p) d -> p c d", p=P)
                pool.dma_start(dst, src).then_inc(w_loaded[i % 2], 16)

            def split_w(i):
                pool.wait_ge(w_loaded[i % 2], 16 * (i // 2 + 1))
                raw, e = w_raw[:, i % 2, :], i % NE
                hi = w1_hi[:, e, :] if i < NE else w2_hi[:, e].rearrange("p c d -> p (c d)")
                lo = w1_lo[:, e, :] if i < NE else w2_lo[:, e].rearrange("p c d -> p (c d)")
                pool.tensor_copy(hi, raw).then_inc(w_hi_made, 1)
                pool.wait_ge(w_hi_made, i + 1)
                pool.tensor_tensor(lo, raw, hi.bitcast(F32), ALU.subtract).then_inc(w_split, 1)
                if i + 2 < 2 * NE:
                    pool.wait_ge(w_split, i + 1)
                    load_w(i + 2)

            for stk in (Q_stack[1], K_stack[1]):
                pool.memset(stk[0:MAX_ROW, :, :].rearrange("p h n -> p (h n)").bitcast(F32), 0.0).then_inc(rows_set, 1)
            for stk in K_stack:
                pool.memset(stk[MAX_ROW:MAX_ROW + 3, :, :].rearrange("p h n -> p (h n)").bitcast(mybir.dt.uint32),
                            TWO_ONES).then_inc(rows_set, 1)
            pool.wait_ge(rows_set, 4)
            load_w(0)
            load_w(1)
            pool.wait_ge(small_loaded, 13 * 16)
            run_slots(pool, slot)

            def add(t, e):
                pool.wait_ge(scaled_made.sem, scaled_made.at(t, e + 1))
                if e > 1:
                    if added.due(t, e - 1):
                        pool.wait_ge(added.sem, added.at(t, e - 1))
                if e == NE - 1:
                    if total_in_psum.due(t - 1, 1):
                        pool.wait_ge(total_in_psum.sem, total_in_psum.at(t - 1, 1))
                dst = total[:].rearrange("p c d -> p (c d)") if e == NE - 1 else acc[:]
                pool.tensor_tensor(dst, acc[:], scaled[:, e % 2, :], ALU.add).then_inc(added.sem, 1)

            def batch(t, before, now):
                if before:
                    add(t - 1, NE - 1)
                if now:
                    for e in range(1, NE - 1):
                        add(t, e)

            run_experts(pool, batch)

        @block.scalar
        def _(act):
            def exps(b, parity, u, js):
                for j in js:
                    n = GROUP * u + j
                    act.wait_ge(score_full.sem, score_full.at(b, n + 1))
                    if j == js[0]:
                        if u >= 2:
                            if pv_done.due(b, u - 1):
                                act.wait_ge(pv_done.sem, pv_done.at(b, u - 1))
                        else:
                            if pv_done.due(b - 1, UNITS - 1 + u):
                                act.wait_ge(pv_done.sem, pv_done.at(b - 1, UNITS - 1 + u))
                    nc.scalar.activation(probs[:, u % 2, j, :], psum[:, bank_of(SCORE, n, parity), :], ACT.Exp,
                                         scale=SCALE).then_inc(exp_done.sem, 1)

            def copy_pv(b, g):
                act.wait_ge(pv_done.sem, pv_done.at(b, 4 * (g + 1)))
                if full["heads"].due(b if g >= 2 else b - 1, g - 1 if g >= 2 else 3 + g):
                    act.wait_ge(full["heads"].sem, full["heads"].at(b if g >= 2 else b - 1, g - 1 if g >= 2 else 3 + g))
                nc.scalar.copy(pv_sb[:, g % 2, :], psum[:, PV, :]).then_inc(pv_copied.sem, 1)

            def take(name, b, parity, g):
                bank = psum[:, SHARED, :]

                def got():
                    act.wait_ge(full[name].sem, full[name].at(b, g + 1))

                if name == "max_rows":
                    got()
                    if m_split.due(b, 3 * g):
                        act.wait_ge(m_split.sem, m_split.at(b, 3 * g))
                    nc.scalar.copy(max_sb[:], bank[0:16, 0:P]).then_inc(taken[name].sem, 1)
                    if m_stored.due(b, 3 * g):
                        act.wait_ge(m_stored.sem, m_stored.at(b, 3 * g))
                    nc.scalar.copy(max_parts[:, 0, :], bank[0:16, 0:P]).then_inc(taken[name].sem, 1)
                elif name == "heads_t":
                    got()
                    if full["project"].due(b - 1, 1):
                        act.wait_ge(full["project"].sem, full["project"].at(b - 1, 1))
                    nc.scalar.copy(heads_t[:], bank).then_inc(taken[name].sem, 1)
                elif name == "normed":
                    got()
                    if full["latent"].due(b - 1, 1):
                        act.wait_ge(full["latent"].sem, full["latent"].at(b - 1, 1))
                    nc.scalar.copy(xn_t[:], bank).then_inc(taken[name].sem, 1)
                elif name == "normed2":
                    got()
                    if full["gate"].due(b - 1, 1):
                        act.wait_ge(full["gate"].sem, full["gate"].at(b - 1, 1))
                    if x2_split.due(b - 1, 1):
                        act.wait_ge(x2_split.sem, x2_split.at(b - 1, 1))
                    nc.scalar.copy(x2_f[:], bank).then_inc(taken[name].sem, 1)
                    nc.scalar.copy(x2_hi[:, tokens(b, 0, C)], bank).then_inc(taken[name].sem, 1)
                elif name == "query":
                    got()
                    if q_split.due(b - 1, 3):
                        act.wait_ge(q_split.sem, q_split.at(b - 1, 3))
                    nc.scalar.activation(q_sb[:], bank, ACT.Identity, bias=bq_sb[:, 0:1]).then_inc(taken[name].sem, 1)
                    if q_stored.due(b - 1, 6):
                        act.wait_ge(q_stored.sem, q_stored.at(b - 1, 6))
                    nc.scalar.activation(q_parts[:, 0, :], bank, ACT.Identity, bias=bq_sb[:, 0:1]).then_inc(taken[name].sem, 1)
                elif name == "key":
                    got()
                    if k_split.due(b - 1, 3):
                        act.wait_ge(k_split.sem, k_split.at(b - 1, 3))
                    nc.scalar.activation(k_sb[:], bank, ACT.Identity, bias=bk_sb[:, 0:1]).then_inc(taken[name].sem, 1)
                    if k_stored.due(b - 1, 6):
                        act.wait_ge(k_stored.sem, k_stored.at(b - 1, 6))
                    nc.scalar.activation(k_parts[:, 0, :], bank, ACT.Identity, bias=bk_sb[:, 0:1]).then_inc(taken[name].sem, 1)
                elif name == "latent":
                    got()
                    if full["value"].due(b - 1, 1):
                        act.wait_ge(full["value"].sem, full["value"].at(b - 1, 1))
                    nc.scalar.activation(lat_t[:], bank[0:LAT, :], ACT.Identity, bias=bl_sb[:, 0:1]).then_inc(taken[name].sem, 1)
                elif name == "gate_t":
                    got()
                    if cw_stored.due(b - 1, 1):
                        act.wait_ge(cw_stored.sem, cw_stored.at(b - 1, 1))
                    nc.scalar.copy(cw_t[:], bank[0:NE, :]).then_inc(taken[name].sem, 1)

            act.wait_ge(small_loaded, 13 * 16)

            def slot(b, parity):
                for u in range(UNITS):
                    for half in range(2):
                        if half == 1 and u % 4 == 0:
                            bb, g = (b, u // 4 - 1) if u else (b - 1, 3)
                            if exists(bb):
                                copy_pv(bb, g)
                        for name, bb, g in steps_at(b, u, half):
                            take(name, bb, parity, g)
                        if (u, half) == (8, 1) and exists(b - 1):
                            if taken["gate"].due(b - 1, 1):
                                act.wait_ge(taken["gate"].sem, taken["gate"].at(b - 1, 1))
                            nc.scalar.activation(g_e[:], g_z[:], ACT.Exp).then_inc(g_exp_done.sem, 1)
                        if exists(b):
                            exps(b, parity, u, (2 * half, 2 * half + 1))

            run_slots(act, slot)

            def batch(t, before, now):
                for n in range(HU if now else 0):
                    act.wait_ge(hidden_full.sem, hidden_full.at(t, n + 1))
                    if n >= 4:
                        if h_lo_made.due(t, n - 3):
                            act.wait_ge(h_lo_made.sem, h_lo_made.at(t, n - 3))
                    else:
                        if h_lo_made.due(t - 1, HU - 3 + n):
                            act.wait_ge(h_lo_made.sem, h_lo_made.at(t - 1, HU - 3 + n))
                    nc.scalar.activation(h_sb[:, n % 4, :], psum[:, HIDDEN[n % 4], :], ACT.Gelu,
                                         bias=b1_sb[:, n:n + 1]).then_inc(gelu_done.sem, 1)

            run_experts(act, batch)

        @block.vector
        def _(dve):
            def clear():
                for stk in (Q_stack[0], K_stack[0]):
                    nc.vector.memset(stk[0:MAX_ROW, :, :].rearrange("p h n -> p (h n)").bitcast(F32), 0.0).then_inc(stack_cleared, 1)

            def ln_stats(b, stats_, made):
                for c in range(C):
                    nc.vector.bn_stats(stats_[:, c, :], X[:, tokens(b, c)]).then_inc(made.sem, 1)
                dve.wait_ge(made.sem, made.at(b, C))

            def ln_aggregate(b, stats_, mv_, mvm):
                for c in range(C):
                    nc.vector.bn_aggr(mv_[:, c, :], stats_[:, c, :]).then_inc(mvm.sem, 1)

            def ln_scale(b, mv_, rstd_, out_, rs, made, transposed):
                dve.wait_ge(rs.sem, rs.at(b, 1))
                if transposed.due(b - 1, 1):
                    dve.wait_ge(transposed.sem, transposed.at(b - 1, 1))
                for c in range(C):
                    nc.vector.tensor_scalar(out_[:, c, :], X[:, tokens(b, c)], mv_[:, c, 0:1], rstd_[:, c:c + 1],
                                            ALU.subtract, ALU.mult).then_inc(made.sem, 1)

            def take(name, b, parity, g):
                bank = psum[:, SHARED, :]
                if name == "heads":
                    view = bank.rearrange("p (c j k) -> p c j k", c=C, j=GROUP)
                    dve.wait_ge(full[name].sem, full[name].at(b, g + 1))
                    nc.vector.reciprocal(inv_sum[:], view[:, :, :, DH]).then_inc(inv_made.sem, 1)
                    dve.wait_ge(inv_made.sem, inv_made.at(b, g + 1))
                    if g == 0:
                        if full["heads_t"].due(b - 1, 1):
                            dve.wait_ge(full["heads_t"].sem, full["heads_t"].at(b - 1, 1))
                    nc.vector.tensor_tensor(heads[:, :, GROUP * g:GROUP * (g + 1), :], view[:, :, :, 0:DH],
                                            inv_sum[:].rearrange("p c (j a) -> p c j a", a=1).to_broadcast([P, C, GROUP, DH]),
                                            ALU.mult).then_inc(taken[name].sem, 1)
                elif name == "value":
                    dve.wait_ge(full[name].sem, full[name].at(b, 1))
                    nc.vector.tensor_tensor(values[:, parity_of(b, parity), :, :, 0:DH],
                                            bank.rearrange("p (c h d) -> p c h d", c=C, h=H),
                                            bv_row[:].rearrange("p (a h d) -> p a h d", a=1, h=H).to_broadcast([P, C, H, DH]),
                                            ALU.add).then_inc(taken[name].sem, 1)
                elif name == "project":
                    dve.wait_ge(full[name].sem, full[name].at(b, 1))
                    dve.wait_ge(bo_added.sem, bo_added.at(b, 1))
                    nc.vector.tensor_tensor(X[:, tokens(b, 0, C)], bank, X[:, tokens(b, 0, C)], ALU.add).then_inc(taken[name].sem, 1)
                    dve.wait_ge(taken[name].sem, taken[name].at(b, 1))
                elif name == "gate":
                    logits = bank[:, 0:C * NE].rearrange("p (c e) -> p c e", c=C)
                    dve.wait_ge(full[name].sem, full[name].at(b, 1))
                    nc.vector.tensor_reduce(g_max[:], logits, AX_X, ALU.max).then_inc(g_max_made.sem, 1)
                    dve.wait_ge(g_max_made.sem, g_max_made.at(b, 1))
                    nc.vector.tensor_tensor(g_z[:], logits, g_max[:].rearrange("p (c a) -> p c a", a=1).to_broadcast([P, C, NE]),
                                            ALU.subtract).then_inc(taken[name].sem, 1)

            def parity_of(b, parity):
                return 1 - parity

            def gate_softmax(b):
                dve.wait_ge(g_exp_done.sem, g_exp_done.at(b, 1))
                nc.vector.tensor_reduce(g_sum[:], g_e[:], AX_X, ALU.add).then_inc(g_sum_made.sem, 1)
                dve.wait_ge(g_sum_made.sem, g_sum_made.at(b, 1))
                nc.vector.reciprocal(g_inv[:], g_sum[:]).then_inc(g_inv_made.sem, 1)
                dve.wait_ge(g_inv_made.sem, g_inv_made.at(b, 1))
                nc.vector.tensor_tensor(g_p[:], g_e[:], g_inv[:].rearrange("p (c a) -> p c a", a=1).to_broadcast([P, C, NE]),
                                        ALU.mult).then_inc(g_p_made.sem, 1)
                dve.wait_ge(g_p_made.sem, g_p_made.at(b, 1))
                own = g_p[:].rearrange("p c (e a) -> p c e a", a=1).to_broadcast([P, C, NE, NE])
                other = g_p[:].rearrange("p c (a f) -> p c a f", a=1).to_broadcast([P, C, NE, NE])
                nc.vector.tensor_tensor(g_ge[:], other, own, ALU.is_ge).then_inc(g_compared.sem, 1)
                nc.vector.tensor_tensor(g_gt[:], other, own, ALU.is_gt).then_inc(g_compared.sem, 1)

            def gate_choice(b):
                dve.wait_ge(g_counted.sem, g_counted.at(b, 1))
                nc.vector.tensor_reduce(g_rank[:], g_ge[:], AX_X, ALU.add).then_inc(g_ranked.sem, 1)
                dve.wait_ge(g_ranked.sem, g_ranked.at(b, 1))
                if full["gate_t"].due(b - 1, 1):
                    dve.wait_ge(full["gate_t"].sem, full["gate_t"].at(b - 1, 1))
                nc.vector.scalar_tensor_tensor(out=cw[:], in0=g_rank[:], scalar=1.5, in1=g_p[:], op0=ALU.is_lt,
                                               op1=ALU.mult).then_inc(cw_made.sem, 1)

            def maxima(b, parity, v, i0):
                g = v // 4
                for i in (i0, i0 + 1):
                    n = GROUP * v + i
                    dve.wait_ge(max_full.sem, max_full.at(b, n + 1))
                    if v % 4 == 0 and i == 0:
                        if g >= 2:
                            if full["max_rows"].due(b, g - 1):
                                dve.wait_ge(full["max_rows"].sem, full["max_rows"].at(b, g - 1))
                        else:
                            if full["max_rows"].due(b - 1, 3 + g):
                                dve.wait_ge(full["max_rows"].sem, full["max_rows"].at(b - 1, 3 + g))
                    nc.vector.tensor_reduce(neg_max[:, g % 2, 4 * (v % 4) + i:4 * (v % 4) + i + 1],
                                            psum[:, bank_of(MAXIMA, n, parity), :], AX_X, ALU.max,
                                            negate=True).then_inc(max_read.sem, 1)

            nc.vector.memset(values[:, 0].rearrange("p c h k -> p (c h k)"), 1.0).then_inc(ones_made, 1)
            nc.vector.memset(values[:, 1].rearrange("p c h k -> p (c h k)"), 1.0).then_inc(ones_made, 1)
            dve.wait_ge(ones_made, 2)
            dve.wait_ge(small_loaded, 13 * 16)

            def slot(b, parity):
                for u in range(UNITS):
                    for half in range(2):
                        if (u, half) == (2, 0) and exists(b + 2):
                            wait_x(dve, b + 2)
                            ln_stats(b + 2, stats, stats_made)
                        if (u, half) == (2, 1) and exists(b + 2):
                            ln_aggregate(b + 2, stats, mv, mv_made)
                        if (u, half) == (4, 0) and exists(b - 1):
                            ln_stats(b - 1, stats2, stats2_made)
                        if (u, half) == (4, 1) and exists(b - 1):
                            ln_aggregate(b - 1, stats2, mv2, mv2_made)
                        if (u, half) == (4, 0) and exists(b + 2):
                            ln_scale(b + 2, mv, rstd, xn, rstd_made, xn_made, full["normed"])
                        if (u, half) == (6, 0) and exists(b - 1):
                            ln_scale(b - 1, mv2, rstd2, xn2, rstd2_made, xn2_made, full["normed2"])
                        if (u, half) == (7, 1) and exists(b - 1):
                            if taken["normed2"].due(b - 1, 2):
                                dve.wait_ge(taken["normed2"].sem, taken["normed2"].at(b - 1, 2))
                            nc.vector.tensor_tensor(x2_lo[:, tokens(b - 1, 0, C)], x2_f[:],
                                                    x2_hi[:, tokens(b - 1, 0, C)].bitcast(F32), ALU.subtract
                                                    ).then_inc(x2_split.sem, 1)
                        for name, bb, g in steps_at(b, u, half):
                            take(name, bb, parity, g)
                        if (u, half) == (9, 0) and exists(b - 1):
                            gate_softmax(b - 1)
                        if (u, half) == (11, 0) and exists(b - 1):
                            gate_choice(b - 1)
                        bb, v = maxima_at(b, u)
                        if exists(bb):
                            maxima(bb, parity if u < UNITS - AHEAD else 1 - parity, v, 2 * half)

            run_slots(dve, slot, clear)
            dve.wait_ge(pv_done.sem, pv_done.at(NB - 1, UNITS))

            def scale(t, e):
                dve.wait_ge(second_done.sem, second_done.at(t, HC * (e + 1)))
                dve.wait_ge(cw_loaded[e].sem, cw_loaded[e].at(t, 1))
                if e == 0:
                    if added.due(t - 1, NE - 1):
                        dve.wait_ge(added.sem, added.at(t - 1, NE - 1))
                elif e >= 3:
                    if added.due(t, e - 2):
                        dve.wait_ge(added.sem, added.at(t, e - 2))
                dst = acc[:] if e == 0 else scaled[:, e % 2, :]
                nc.vector.scalar_tensor_tensor(out=dst, in0=psum[:, EXPERT_OUT[e % 2], :], scalar=b2_sb[:, e:e + 1],
                                               in1=cw_row[:, e, :], op0=ALU.add, op1=ALU.mult).then_inc(scaled_made.sem, 1)

            def finish(t):
                dve.wait_ge(total_in_psum.sem, total_in_psum.at(t, 1))
                if result_stored.due(t - 1, 1):
                    dve.wait_ge(result_stored.sem, result_stored.at(t - 1, 1))
                nc.vector.tensor_tensor(result[:].rearrange("p c d -> p (c d)"), psum[:, SHARED, :], X[:, tokens(t, 0, C)],
                                        ALU.add).then_inc(result_made.sem, 1)

            def batch(t, before, now):
                for n in range(HU if now else 8):
                    if now:
                        dve.wait_ge(gelu_done.sem, gelu_done.at(t, n + 1))
                        if n >= 4:
                            if second_done.due(t, n - 3):
                                dve.wait_ge(second_done.sem, second_done.at(t, n - 3))
                        else:
                            if second_done.due(t - 1, HU - 3 + n):
                                dve.wait_ge(second_done.sem, second_done.at(t - 1, HU - 3 + n))
                        nc.vector.tensor_copy(h_hi[:, n % 4, :], h_sb[:, n % 4, :]).then_inc(h_hi_made.sem, 1)
                        dve.wait_ge(h_hi_made.sem, h_hi_made.at(t, n + 1))
                        nc.vector.tensor_tensor(h_lo[:, n % 4, :], h_sb[:, n % 4, :], h_hi[:, n % 4, :].bitcast(F32),
                                                ALU.subtract).then_inc(h_lo_made.sem, 1)
                    if n == 2 and before:
                        scale(t - 1, NE - 1)
                    if n == 7 and before:
                        finish(t - 1)
                    if now and n >= 6 and (n - 6) % 4 == 0:
                        scale(t, (n - 6) // 4)

            run_experts(dve, batch)

        @block.tensor
        def _(pe):
            def shared_bank_free(b, u, half, index):
                for name, bb, g in reversed(order_before(b, index)):
                    pe.wait_ge(taken[name].sem, taken[name].at(bb, READS.get(name, 1) * (g + 1)))
                    return

            def order_before(b, index):
                found = [(n, b - 1 + db, g) for _, _, n, db, g in STEPS if exists(b - 1 + db)]
                return found + [(n, b + db, g) for _, _, n, db, g in STEPS[:index] if exists(b + db)]

            def step(name, b, parity, g):
                bank = psum[:, SHARED, :]

                def transposes(src, n, rows):
                    for c in range(n):
                        mm = pe.transpose(bank[:, c * P:(c + 1) * P], src(c), ident[:])
                    return mm

                if name == "max_rows":
                    pe.wait_ge(max_read.sem, max_read.at(b, 16 * (g + 1)))
                    mm = pe.transpose(bank[0:16, 0:P], neg_max[:, g % 2, :], ident[:])
                elif name == "heads":
                    pe.wait_ge(pv_copied.sem, pv_copied.at(b, g + 1))
                    mm = transposes(lambda c: pv_sb[:, g % 2, c * P:(c + 1) * P], C, P)
                elif name == "heads_t":
                    pe.wait_ge(taken["heads"].sem, taken["heads"].at(b, GROUP))
                    mm = transposes(lambda c: heads[:, c].rearrange("p h d -> p (h d)"), C, P)
                elif name == "project":
                    pe.wait_ge(taken["heads_t"].sem, taken["heads_t"].at(b, 1))
                    for c in range(C):
                        mm = pe.matmul(bank[:, c * P:(c + 1) * P], heads_t[:, c * P:(c + 1) * P], wo_sb[:], start=True, stop=True)
                elif name == "normed":
                    pe.wait_ge(xn_made.sem, xn_made.at(b, C))
                    mm = transposes(lambda c: xn[:, c], C, P)
                elif name == "normed2":
                    pe.wait_ge(xn2_made.sem, xn2_made.at(b, C))
                    mm = transposes(lambda c: xn2[:, c], C, P)
                elif name == "query":
                    pe.wait_ge(taken["normed"].sem, taken["normed"].at(b, 1))
                    mm = pe.matmul(bank, wq_sb[:], xn_t[:], start=True, stop=True)
                elif name == "latent":
                    mm = pe.matmul(bank[0:LAT, :], wl_sb[:], xn_t[:], start=True, stop=True)
                elif name == "key":
                    pe.wait_ge(taken["latent"].sem, taken["latent"].at(b, 1))
                    mm = pe.matmul(bank, wk_sb[:], lat_t[:], start=True, stop=True)
                elif name == "value":
                    for c in range(C):
                        mm = pe.matmul(bank[:, c * P:(c + 1) * P], lat_t[:, c * P:(c + 1) * P], wv_sb[:], start=True, stop=True)
                elif name == "gate":
                    pe.wait_ge(taken["normed2"].sem, taken["normed2"].at(b, 2))
                    for c in range(C):
                        mm = pe.matmul(bank[:, c * NE:(c + 1) * NE], x2_f[:, c * P:(c + 1) * P], wg_sb[:], start=True, stop=True)
                elif name == "gate_t":
                    pe.wait_ge(cw_made.sem, cw_made.at(b, 1))
                    for c in range(C):
                        mm = pe.transpose(bank[0:NE, c * P:(c + 1) * P], cw[:, c], ident[:])
                mm.then_inc(full[name].sem, 1)

            def scores(b, parity, u, js):
                g, kc = u // 4, u % 4
                for j in js:
                    n, h = GROUP * u + j, GROUP * g + j
                    bb, k = bank_freed(SCORE, n, b, parity)
                    if exp_done.due(bb, k):
                        pe.wait_ge(exp_done.sem, exp_done.at(bb, k))
                    if kc == 0 and j == 0:
                        pe.wait_ge(stacked[g].sem, stacked[g].at(b, 2))
                        pe.wait_ge(m_stored.sem, m_stored.at(b, 3 * (g + 1)))
                    pe.matmul(psum[:, bank_of(SCORE, n, parity), :],
                              K_stack[parity][0:MAX_ROW + 3, h, kc * P:(kc + 1) * P],
                              Q_stack[parity][0:MAX_ROW + 3, h, :], start=True, stop=True).then_inc(score_full.sem, 1)

            def score_rows(b, parity, v, i0):
                for i in (i0, i0 + 1):
                    n = GROUP * v + i
                    bb, k = bank_freed(MAXIMA, n, b, parity)
                    if max_read.due(bb, k):
                        pe.wait_ge(max_read.sem, max_read.at(bb, k))
                    if v % 4 == 0 and i == 0:
                        pe.wait_ge(stacked[v // 4].sem, stacked[v // 4].at(b, 2))
                    pe.matmul(psum[:, bank_of(MAXIMA, n, parity), :],
                              Q_stack[parity][0:MAX_ROW, v, i * P:(i + 1) * P],
                              K_stack[parity][0:MAX_ROW, v, :], start=True, stop=True).then_inc(max_full.sem, 1)

            def weighted(b, parity, u):
                g, kc = u // 4, u % 4
                pe.wait_ge(exp_done.sem, exp_done.at(b, GROUP * (u + 1)))
                if u == 0:
                    pe.wait_ge(taken["value"].sem, taken["value"].at(b, 1))
                if kc == 0:
                    bb, k = (b, g) if g else (b - 1, GROUP)
                    if pv_copied.due(bb, k):
                        pe.wait_ge(pv_copied.sem, pv_copied.at(bb, k))
                for j in range(GROUP):
                    mm = pe.matmul(psum[32 * j:32 * (j + 1), PV, :], values[:, parity, kc, GROUP * g + j, :],
                                   probs[:, u % 2, j, :], start=(kc == 0), stop=(kc == C - 1))
                mm.then_inc(pv_done.sem, 1)

            pe.wait_ge(small_loaded, 13 * 16)
            pe.wait_ge(consts_made, 8)
            pe.wait_ge(ones_made, 2)

            def slot(b, parity):
                for u in range(UNITS):
                    for half in range(2):
                        for index, (v, w, name, db, g) in enumerate(STEPS):
                            if (v, w) == (u, half) and exists(b + db):
                                shared_bank_free(b, u, half, index)
                                step(name, b + db, parity, g)
                        if exists(b):
                            scores(b, parity, u, (2 * half, 2 * half + 1))
                        bb, v = maxima_at(b, u)
                        if exists(bb):
                            score_rows(bb, parity if u < UNITS - AHEAD else 1 - parity, v, 2 * half)
                        if half == 0:
                            if u and exists(b):
                                weighted(b, parity, u - 1)
                            if not u and exists(b - 1):
                                weighted(b - 1, 1 - parity, UNITS - 1)

            pe.wait_ge(rows_set, 4)
            run_slots(pe, slot, lambda: pe.wait_ge(stack_cleared, 2))
            pe.wait_ge(taken["gate_t"].sem, taken["gate_t"].at(NB - 1, 1))
            pe.wait_ge(exp_done.sem, exp_done.at(NB - 1, NT))
            pe.wait_ge(max_read.sem, max_read.at(NB - 1, NT))

            def first(t, n):
                e, c = n // HC, n % HC
                if n >= 4:
                    if gelu_done.due(t, n - 3):
                        pe.wait_ge(gelu_done.sem, gelu_done.at(t, n - 3))
                else:
                    if gelu_done.due(t - 1, HU - 3 + n):
                        pe.wait_ge(gelu_done.sem, gelu_done.at(t - 1, HU - 3 + n))
                if isinstance(t, int) and t == 0 and c == 0:
                    pe.wait_ge(w_split, e + 1)
                if n == 0 and isinstance(t, int) and t == 0:
                    pe.wait_ge(x2_split.sem, x2_split.at(NB - 1, 1))
                cols = slice(c * P, (c + 1) * P)
                bank = psum[:, HIDDEN[n % 4], :]
                pe.matmul(bank, w1_hi[:, e, cols], x2_hi[:, tokens(t, 0, C)], start=True, stop=False)
                pe.matmul(bank, w1_hi[:, e, cols], x2_lo[:, tokens(t, 0, C)], start=False, stop=False)
                pe.matmul(bank, w1_lo[:, e, cols], x2_hi[:, tokens(t, 0, C)], start=False, stop=True).then_inc(hidden_full.sem, 1)

            def second(t, n):
                e, c = n // HC, n % HC
                pe.wait_ge(h_lo_made.sem, h_lo_made.at(t, n + 1))
                if isinstance(t, int) and t == 0 and c == 0:
                    pe.wait_ge(w_split, NE + e + 1)
                if c == 0:
                    if e >= 2:
                        if scaled_made.due(t, e - 1):
                            pe.wait_ge(scaled_made.sem, scaled_made.at(t, e - 1))
                    else:
                        if scaled_made.due(t - 1, NE - 1 + e):
                            pe.wait_ge(scaled_made.sem, scaled_made.at(t - 1, NE - 1 + e))
                bank = psum[:, EXPERT_OUT[e % 2], :]
                pe.matmul(bank, w2_hi[:, e, c, :], h_hi[:, n % 4, :], start=(c == 0), stop=False)
                pe.matmul(bank, w2_hi[:, e, c, :], h_lo[:, n % 4, :], start=False, stop=False)
                pe.matmul(bank, w2_lo[:, e, c, :], h_hi[:, n % 4, :], start=False, stop=(c == HC - 1)).then_inc(second_done.sem, 1)

            def batch(t, before, now):
                for n in range(HU if now else 8):
                    if now:
                        first(t, n)
                    if n < LAG:
                        if before:
                            second(t - 1, HU - LAG + n)
                    elif now:
                        second(t, n - LAG)
                    if n == 6 and before:
                        if added.due(t - 1, NE - 1):
                            pe.wait_ge(added.sem, added.at(t - 1, NE - 1))
                        if result_made.due(t - 2, 1):
                            pe.wait_ge(result_made.sem, result_made.at(t - 2, 1))
                        for c in range(C):
                            mm = pe.transpose(psum[:, SHARED, c * P:(c + 1) * P], total[:, c], ident[:])
                        mm.then_inc(total_in_psum.sem, 1)

            run_experts(pe, batch)


def kernel(**inputs):
    import numpy as _np
    import concourse.bacc as _bacc
    from concourse import mybir as _mybir
    from concourse.bass_utils import run_bass_kernel_spmd as _run

    def arr(name):
        return _np.ascontiguousarray(inputs[name])

    x, b1 = arr("L0_attn_x"), arr("L0_ffn_b1")
    laid_out = {
        "x": x, "wq": arr("L0_attn_Wq"), "bq": arr("L0_attn_bq"), "wl": arr("L0_attn_Wl"), "bl": arr("L0_attn_bl"),
        "wk": arr("L0_attn_Wk"), "bk": arr("L0_attn_bk"), "wv": arr("L0_attn_Wv"), "bv": arr("L0_attn_bv"),
        "wo": arr("L0_attn_Wo"), "bo": arr("L0_attn_bo"),
        "w_gate_t": _np.ascontiguousarray(arr("L0_ffn_w_gate").T), "w1": arr("L0_ffn_W1"),
        "b1_t": _np.ascontiguousarray(b1.reshape(-1, 128).T), "w2": arr("L0_ffn_W2"),
        "b2_t": _np.ascontiguousarray(arr("L0_ffn_b2").T),
    }
    nc = _bacc.Bacc("TRN2", target_bir_lowering=False, num_devices=1)
    args = {n: nc.dram_tensor(f"in_{n}", a.shape, _mybir.dt.from_np(a.dtype), kind="ExternalInput").ap()
            for n, a in laid_out.items()}
    out = nc.dram_tensor("out_0", x.shape, _mybir.dt.from_np(x.dtype), kind="ExternalOutput").ap()
    block_attention_moe(nc, **args, out=out)
    r = _run(nc, [{f"in_{n}": a for n, a in laid_out.items()}], core_ids=[0])
    return r.results[0]["out_0"]
```

```python
from contextlib import ExitStack, nullcontext

import concourse.bass as bass
from concourse import mybir

ALU = mybir.AluOpType
ACT = mybir.ActivationFunctionType
F32 = mybir.dt.float32
F32R = mybir.dt.float32r
BF16 = mybir.dt.bfloat16
AX_X = mybir.AxisListType.X

P = 128
TWO_ONES = 0x3F803F80
EARLY, LATE = 9, 4
LN_EPS = 1e-5

UNITS = 16
AHEAD = 8
GROUP = 4
ROWS = 48
MAX_ROW = 96

STEPS = [
    (1, 0, "heads", -1, 3), (1, 1, "max_rows", 0, 1), (2, 0, "heads_t", -1, 0), (3, 0, "project", -1, 0),
    (4, 0, "value", 1, 0), (5, 0, "heads", 0, 0), (5, 1, "max_rows", 0, 2), (6, 0, "normed", 2, 0),
    (6, 1, "query", 2, 0), (7, 0, "normed2", -1, 0), (7, 1, "latent", 2, 0), (8, 0, "gate", -1, 0),
    (8, 1, "max_rows", 0, 3), (9, 0, "key", 2, 0), (11, 0, "heads", 0, 1), (12, 1, "max_rows", 1, 0),
    (13, 0, "gate_t", -1, 0), (14, 0, "heads", 0, 2),
]
PER_BATCH = {"max_rows": 4, "heads": 4}
READS = {"max_rows": 2, "query": 2, "key": 2, "normed2": 2}
STEP_NAMES = sorted({s[2] for s in STEPS})


class Signal:

    def __init__(self, sem, per_batch, by=1):
        self.sem, self.per_batch, self.by = sem, per_batch, by

    def at(self, b, k):
        return b * (self.per_batch * self.by) + k * self.by

    def due(self, b, k):
        return not isinstance(b, int) or self.at(b, k) > 0


def block_attention_moe(nc, x, wq, bq, wl, bl, wk, bk, wv, bv, wo, bo, w_gate_t, w1, b1_t, w2, b2_t, out):
    NB, S, D = x.shape
    NE, _, F = w1.shape
    LAT = wl.shape[1]
    H, DH = 16, 8
    assert H * DH == D == P and S == 4 * P
    C = S // P
    HC = F // P
    SCALE = float(DH) ** -0.5
    NT = UNITS * GROUP
    HU = NE * HC
    LAG = 3

    ctx = ExitStack()
    with ctx:
        def sb(name, shape, dt=F32):
            return ctx.enter_context(nc.sbuf_tensor(name, shape, dt))

        def sem(name):
            return ctx.enter_context(nc.semaphore(name))

        def signal(name, per_batch, by=1):
            return Signal(sem(name), per_batch, by)

        psum = ctx.enter_context(nc.psum_tensor("psum", [P, 8, S], F32))
        SCORE, MAXIMA, PV, SHARED = (0, 1, 2), (3, 4, 5), 6, 7
        HIDDEN, EXPERT_OUT = (0, 1, 2, 3), (4, 5)

        X = sb("X", [P, NB * S])
        x2_hi = sb("x2_hi", [P, NB * S], F32R)
        x2_lo = sb("x2_lo", [P, NB * S], F32R)
        ident = sb("ident", [P, P])
        wq_sb, wo_sb = sb("wq_sb", [P, D]), sb("wo_sb", [P, D])
        wl_sb, wk_sb, wv_sb = sb("wl_sb", [P, LAT]), sb("wk_sb", [LAT, D]), sb("wv_sb", [LAT, D])
        wg_sb, b1_sb, b2_sb = sb("wg_sb", [P, NE]), sb("b1_sb", [P, HU]), sb("b2_sb", [P, NE])
        bq_sb, bk_sb, bl_sb = sb("bq_sb", [P, 1]), sb("bk_sb", [P, 1]), sb("bl_sb", [LAT, 1])
        bv_row, bo_row = sb("bv_row", [P, D]), sb("bo_row", [P, D])
        earlier, later = sb("earlier", [P, NE, NE]), sb("later", [P, NE, NE])
        minus_half, eps = sb("minus_half", [P, C]), sb("eps", [P, C])

        stack_base = -(-nc.sbuf_base // 32) * 32
        Q_stack = [sb(f"Q_stack{i}", [P, H, S], BF16) for i in range(2)]
        K_stack = [sb(f"K_stack{i}", [P, H, S], BF16) for i in range(2)]
        probs = sb("probs", [P, 2, GROUP, S])
        values = sb("values", [P, 2, C, H, 32])
        pv_sb = sb("pv_sb", [P, 2, S])
        xn, xn2 = sb("xn", [P, C, D]), sb("xn2", [P, C, D])
        w2_raw_base = -(-nc.sbuf_base // 32) * 32
        xn_hi, lat_t = sb("xn_hi", [P, S], F32R), sb("lat_t", [LAT, S])
        q_sb, k_sb, rest = sb("q_sb", [P, S]), sb("k_sb", [P, S]), sb("rest", [P, S])
        q_parts, k_parts = sb("q_parts", [P, 3, S], BF16), sb("k_parts", [P, 3, S], BF16)
        heads, heads_t, x2_f = sb("heads", [P, C, H, DH]), sb("heads_t", [P, S]), sb("x2_f", [P, S])
        inv_sum = sb("inv_sum", [P, C, GROUP])
        stats, mv, rstd = sb("stats", [P, C, 6]), sb("mv", [P, C, 2]), sb("rstd", [P, C])
        stats2, mv2, rstd2 = sb("stats2", [P, C, 6]), sb("mv2", [P, C, 2]), sb("rstd2", [P, C])
        neg_max = sb("neg_max", [P, 2, 16])
        max_sb, max_rest = sb("max_sb", [16, P]), sb("max_rest", [16, P])
        max_parts = sb("max_parts", [16, 3, P], BF16)
        g_max, g_sum, g_inv = sb("g_max", [P, C]), sb("g_sum", [P, C]), sb("g_inv", [P, C])
        g_z, g_e, g_p = sb("g_z", [P, C, NE]), sb("g_e", [P, C, NE]), sb("g_p", [P, C, NE])
        g_ge, g_gt = sb("g_ge", [P, C, NE, NE]), sb("g_gt", [P, C, NE, NE])
        g_rank, cw, cw_t = sb("g_rank", [P, C, NE]), sb("cw", [P, C, NE]), sb("cw_t", [NE, S])

        size = H * S * 2
        h_at = -(-nc.sbuf_base // 32) * 32
        h_sb = sb("h_sb", [P, 4, S])
        scaled_at = -(-nc.sbuf_base // 32) * 32
        scaled, acc, total = sb("scaled", [P, 2, S]), sb("acc", [P, S]), sb("total", [P, C, P])
        result = sb("result", [P, C, D])
        w_raw = sb("w_raw", [P, 2, F])

        def over(name, shape, dt, offset):
            return nc.alloc_sbuf_tensor_at(name, shape, dt, offset=offset)

        xn_lo = over("xn_lo", [P, S], F32R, h_at)
        wq_hi = over("wq_hi", [P, D], F32R, scaled_at)
        wq_lo = over("wq_lo", [P, D], F32R, scaled_at + D * 4)
        wl_hi = over("wl_hi", [P, LAT], F32R, scaled_at + 2 * D * 4)
        wl_lo = over("wl_lo", [P, LAT], F32R, scaled_at + (2 * D + LAT) * 4)
        w2_raw = over("w2_raw", [P, NE, HC, D], F32, w2_raw_base)
        w1_hi = over("w1_hi", [P, NE, F], F32R, stack_base)
        w2_hi = over("w2_hi", [P, NE, HC, D], F32R, stack_base + size)
        w1_lo = over("w1_lo", [P, NE, F], F32R, stack_base + 2 * size)
        w2_lo = over("w2_lo", [P, NE, HC, D], F32R, stack_base + 3 * size)
        h_hi = over("h_hi", [P, 4, S], F32R, stack_base + 4 * size)
        h_lo = over("h_lo", [P, 4, S], F32R, stack_base + 4 * size + 4 * S * 4)
        cw_row = over("cw_row", [P, NE, S], F32, stack_base + 4 * size + 8 * S * 4)

        q_dram = nc.dram_tensor("q_dram", [2, H, ROWS, S], BF16).ap()
        k_dram = nc.dram_tensor("k_dram", [2, H, ROWS, S], BF16).ap()
        cw_dram = nc.dram_tensor("cw_dram", [NB * NE, S], F32).ap()

        x_loaded = [sem(f"x_loaded{i}") for i in range(3)]
        small_loaded, late_loaded = sem("small_loaded"), sem("late_loaded")
        consts_made = sem("consts_made")
        fill_made, rows_filled = sem("fill_made"), sem("rows_filled")
        ones_made = sem("ones_made")
        full = {n: signal(f"{n}_in_psum", PER_BATCH.get(n, 1)) for n in STEP_NAMES}
        taken = {n: signal(f"{n}_taken", READS.get(n, 1) * PER_BATCH.get(n, 1)) for n in STEP_NAMES}
        score_full, exp_done = signal("score_full", NT), signal("exp_done", NT)
        max_full, max_read = signal("max_full", NT), signal("max_read", NT)
        pv_done, pv_copied = signal("pv_done", UNITS), signal("pv_copied", GROUP)
        stats_made, mv_made = signal("stats_made", C), signal("mv_made", C)
        var_made, rstd_made, xn_made = signal("var_made", 1), signal("rstd_made", 1), signal("xn_made", 1)
        centred, centred2 = signal("centred", 1), signal("centred2", 1)
        stats2_made, mv2_made = signal("stats2_made", C), signal("mv2_made", C)
        var2_made, rstd2_made, xn2_made = signal("var2_made", 1), signal("rstd2_made", 1), signal("xn2_made", 1)
        bo_added, residual_made = signal("bo_added", 1), signal("residual_made", 1)
        q_split, k_split, m_split = signal("q_split", 3), signal("k_split", 3), signal("m_split", 12)
        q_stored, k_stored = signal("q_stored", 6, 16), signal("k_stored", 6, 16)
        stacked = [signal(f"stacked{g}", 2, 16) for g in range(4)]
        m_stored = signal("m_stored", 12, 16)
        inv_made = signal("inv_made", 4)
        x2_split = signal("x2_split", 1)
        g_max_made, g_exp_done, g_sum_made = signal("g_max_made", 1), signal("g_exp_done", 1), signal("g_sum_made", 1)
        g_inv_made, g_p_made, g_compared = signal("g_inv_made", 1), signal("g_p_made", 1), signal("g_compared", 2)
        g_masked, g_counted, g_ranked = signal("g_masked", 2), signal("g_counted", 1), signal("g_ranked", 1)
        cw_made, cw_stored = signal("cw_made", 1), signal("cw_stored", 1, 16)
        w_loaded = [sem(f"w_loaded{i}") for i in range(2)]
        xn_hi_made = signal("xn_hi_made", 1)
        proj_hi_made, proj_split = sem("proj_hi_made"), sem("proj_split")
        w2_loaded, w2_hi_made = sem("w2_loaded"), sem("w2_hi_made")
        w1_hi_made, w1_split, w2_split = sem("w1_hi_made"), sem("w1_split"), sem("w2_split")
        hidden_full, gelu_done = signal("hidden_full", HU), signal("gelu_done", HU)
        h_hi_made, h_lo_made = signal("h_hi_made", HU), signal("h_lo_made", HU)
        second_done = signal("second_done", HU)
        scaled_made, added = signal("scaled_made", NE), signal("added", NE - 1)
        cw_loaded = [signal(f"cw_loaded{e}", 1, 16) for e in range(NE)]
        total_in_psum, result_made = signal("total_in_psum", 1), signal("result_made", 1)
        result_stored = signal("result_stored", 1, 16)

        block = ctx.enter_context(nc.Block())

        def exists(b):
            return not isinstance(b, int) or 0 <= b < NB

        def run_slots(eng, slot, after_first=lambda: None):
            slot(-2, 0)
            after_first()
            for b in (-1, 0, 1):
                slot(b, b % 2)
            with eng.Fori(2, 5, 2) as b:
                slot(b, 0)
                slot(b + 1, 1)
            for b in range(6, NB):
                slot(b, b % 2)

        def run_experts(eng, batch):
            batch(0, False, True)
            batch(1, True, True)
            with eng.Fori(2, NB - 1) as t:
                batch(t, True, True)
            batch(NB - 1, True, True)
            batch(NB, True, False)

        def steps_at(b, u, half):
            return [(n, b + db, g) for v, w, n, db, g in STEPS if (v, w) == (u, half) and exists(b + db)]

        def maxima_at(b, u):
            return (b, u + AHEAD) if u < UNITS - AHEAD else (b + 1, u + AHEAD - UNITS)

        def bank_of(banks, n, parity):
            return banks[(n + parity) % len(banks)]

        def bank_freed(banks, n, b, parity):
            if n >= len(banks):
                return b, n - len(banks) + 1
            before = max(m for m in range(NT) if bank_of(banks, m, 1 - parity) == bank_of(banks, n, parity))
            return b - 1, before + 1

        def wait_x(eng, b):
            eng.wait_ge(x_loaded[min(b, 2)] if isinstance(b, int) else x_loaded[2],
                        16 if isinstance(b, int) and b < 2 else 16 * (NB - 2))

        def tokens(b, c=0, n=1):
            return bass.ds(b * S + c * P, n * P)

        @block.sync
        def _(sp):
            def load_x(b):
                sp.dma_start(X[:, tokens(b, 0, C)].rearrange("p (c d) -> p c d", c=C),
                             x[b].rearrange("(c p) d -> p c d", p=P)).then_inc(x_loaded[min(b, 2)], 16)

            def column(v):
                return v.rearrange("(p a) -> p a", a=1)

            def fill_rows(parity):
                for stk in (Q_stack[parity], K_stack[parity]):
                    sp.dma_start(stk[ROWS:MAX_ROW, :, :].rearrange("p (a h) n -> p a (h n)", h=2),
                                 w_raw[ROWS:MAX_ROW, 0:1, :].bitcast(BF16).to_broadcast([MAX_ROW - ROWS, H // 2, 2 * S])
                                 ).then_inc(rows_filled, 16)
                sp.dma_start(K_stack[parity][MAX_ROW:MAX_ROW + 3, :, :].rearrange("p (a h) n -> p a (h n)", h=2),
                             w_raw[MAX_ROW:MAX_ROW + 3, 1:2, :].bitcast(BF16).to_broadcast([3, H // 2, 2 * S])
                             ).then_inc(rows_filled, 16)

            load_x(0)
            early = ((wq_sb, wq), (bq_sb, column(bq)), (wl_sb, wl), (bl_sb, column(bl)), (wk_sb, wk), (bk_sb, column(bk)),
                     (bo_row, bo.partition_broadcast(P)), (wv_sb, wv), (bv_row, bv.partition_broadcast(P)))
            assert len(early) == EARLY
            for dst, src in early:
                sp.dma_start(dst[:], src).then_inc(small_loaded, 16)
            load_x(1)
            sp.wait_ge(fill_made, 2)
            fill_rows(0)
            late = ((wo_sb, wo), (wg_sb, w_gate_t), (b1_sb, b1_t), (b2_sb, b2_t))
            assert len(late) == LATE
            for dst, src in late:
                sp.dma_start(dst[:], src).then_inc(late_loaded, 16)
            fill_rows(1)
            for b in range(2, NB):
                load_x(b)

            def stack(b, parity, g):
                hs = slice(GROUP * g, GROUP * (g + 1))
                for stk, dram in ((Q_stack, q_dram), (K_stack, k_dram)):
                    sp.dma_start(stk[parity][0:ROWS, hs, :],
                                 dram[parity, hs].rearrange("h r n -> r h n")).then_inc(stacked[g].sem, 16)

            def store_parts(b, parity):
                for parts, order, dram, ready, stored in ((q_parts, (0, 0, 0, 1, 1, 2), q_dram, q_split, q_stored),
                                                          (k_parts, (0, 1, 2, 0, 1, 0), k_dram, k_split, k_stored)):
                    sp.wait_ge(ready.sem, ready.at(b, 3))
                    for r, part in enumerate(order):
                        sp.dma_start(dram[parity, :, r * DH:(r + 1) * DH, :], parts[:, part, :]).then_inc(stored.sem, 16)
                sp.wait_ge(q_stored.sem, q_stored.at(b, 6))
                sp.wait_ge(k_stored.sem, k_stored.at(b, 6))

            def max_rows(b, parity, g):
                sp.wait_ge(m_split.sem, m_split.at(b, 3 * (g + 1)))
                for part in range(3):
                    sp.dma_start(Q_stack[parity][MAX_ROW + part:MAX_ROW + part + 1, GROUP * g:GROUP * (g + 1), :],
                                 max_parts[:, part, :]).then_inc(m_stored.sem, 16)

            def place(b, parity, u, half):
                for name, bb, g in steps_at(b, u, half):
                    if name == "max_rows":
                        max_rows(bb, parity if u < 12 else 1 - parity, g)
                    if name == "gate_t":
                        sp.wait_ge(taken["gate_t"].sem, taken["gate_t"].at(bb, 1))
                        sp.dma_start(cw_dram[bass.ds(bb * NE, NE), :], cw_t[:]).then_inc(cw_stored.sem, 16)

            def slot(b, parity):
                if exists(b + 1):
                    if score_full.due(b - 1, NT):
                        sp.wait_ge(score_full.sem, score_full.at(b - 1, NT))
                    stack(b + 1, 1 - parity, 3)
                for u in range(UNITS):
                    if u == 13:
                        if exists(b + 2):
                            store_parts(b + 2, parity)
                            for g in (0, 1, 2):
                                if exists(b):
                                    sp.wait_ge(score_full.sem, score_full.at(b, 16 * (g + 1)))
                                stack(b + 2, parity, g)
                    for half in range(2):
                        place(b, parity, u, half)
                    if u == 1 and isinstance(b, int) and b == NB - 1:
                        sp.wait_ge(taken["value"].sem, taken["value"].at(NB - 1, 1))
                        sp.dma_start(w2_raw[:].rearrange("p e c d -> p (e c) d"),
                                     w2.rearrange("e (c p) d -> p (e c) d", p=P)).then_inc(w2_loaded, 16)

            run_slots(sp, slot)

            sp.wait_ge(pv_done.sem, pv_done.at(NB - 1, UNITS))
            sp.wait_ge(cw_stored.sem, cw_stored.at(NB - 2, 1))
            for e in range(NE):
                sp.dma_start(cw_row[:, e, :], cw_dram[e].partition_broadcast(P)).then_inc(cw_loaded[e].sem, 16)

            def batch(t, before, now):
                for s in range(HU if now else 8):
                    if isinstance(t, int) and t == 0:
                        place(NB, 0, s // 2, s % 2)
                    if s == 2 and before and now:
                        if scaled_made.due(t - 1, NE):
                            sp.wait_ge(scaled_made.sem, scaled_made.at(t - 1, NE))
                        sp.dma_start(cw_row[:, NE - 1, :],
                                     cw_dram[t * NE + (NE - 1)].partition_broadcast(P)
                                     if isinstance(t, int) else
                                     cw_dram[bass.ds(t * NE + (NE - 1), 1), :].rearrange("a n -> (a n)").partition_broadcast(P)
                                     ).then_inc(cw_loaded[NE - 1].sem, 16)
                    if s == 7 and before:
                        if result_made.due(t - 1, 1):
                            sp.wait_ge(result_made.sem, result_made.at(t - 1, 1))
                        sp.dma_start(out[bass.ds(t - 1, 1)].rearrange("a (c p) d -> p (a c) d", p=P),
                                     result[:]).then_inc(result_stored.sem, 16)
                    if now and s >= 6 and (s - 6) % 4 == 0 and not (isinstance(t, int) and t + 1 >= NB):
                        e = (s - 6) // 4
                        sp.wait_ge(scaled_made.sem, scaled_made.at(t, e + 1))
                        if isinstance(t, int):
                            src = cw_dram[(t + 1) * NE + e]
                        else:
                            src = cw_dram[bass.ds((t + 1) * NE + e, 1), :].rearrange("a n -> (a n)")
                        sp.dma_start(cw_row[:, e, :], src.partition_broadcast(P)).then_inc(cw_loaded[e].sem, 16)

                if isinstance(t, int) and t == 0:
                    sp.wait_ge(cw_stored.sem, cw_stored.at(NB - 1, 1))

            run_experts(sp, batch)
            sp.wait_ge(result_stored.sem, result_stored.at(NB - 1, 1))

        @block.gpsimd
        def _(pool):
            pool.memset(ident[:], 0.0).then_inc(consts_made, 1)
            pool.memset(earlier[:], 1.0).then_inc(consts_made, 1)
            pool.memset(later[:], 1.0).then_inc(consts_made, 1)
            pool.memset(minus_half[:], -0.5).then_inc(consts_made, 1)
            pool.memset(eps[:], LN_EPS).then_inc(consts_made, 1)
            pool.wait_ge(consts_made, 5)
            pool.affine_select(out=ident[:], in_=ident[:], compare_op=ALU.not_equal, fill=1.0, base=0,
                               pattern=[[-1, P]], channel_multiplier=1).then_inc(consts_made, 1)
            pool.affine_select(out=earlier[:], in_=earlier[:], compare_op=ALU.is_gt, fill=0.0, base=0,
                               pattern=[[1, NE], [-1, NE]], channel_multiplier=0).then_inc(consts_made, 1)
            pool.affine_select(out=later[:], in_=later[:], compare_op=ALU.is_gt, fill=0.0, base=0,
                               pattern=[[-1, NE], [1, NE]], channel_multiplier=0).then_inc(consts_made, 1)
            pool.wait_ge(consts_made, 8)

            def normalise(b, mv_, rstd_, out_, mvm, var, rs, centred, made, transposed):
                pool.wait_ge(mvm.sem, mvm.at(b, C))
                if transposed.due(b - 1, 1):
                    pool.wait_ge(transposed.sem, transposed.at(b - 1, 1))
                pool.tensor_tensor(rstd_[:], mv_[:, :, 1], eps[:], ALU.add).then_inc(var.sem, 1)
                pool.tensor_tensor(out_[:], X[:, tokens(b, 0, C)].rearrange("p (c d) -> p c d", c=C),
                                   mv_[:, :, 0:1].to_broadcast([P, C, D]), ALU.subtract).then_inc(centred.sem, 1)
                pool.wait_ge(var.sem, var.at(b, 1))
                pool.tensor_tensor(rstd_[:], rstd_[:], minus_half[:], ALU.pow).then_inc(rs.sem, 1)
                pool.wait_ge(centred.sem, centred.at(b, 1))
                pool.wait_ge(rs.sem, rs.at(b, 1))
                pool.tensor_tensor(out_[:], out_[:], rstd_[:].rearrange("p (c a) -> p c a", a=1).to_broadcast([P, C, D]),
                                   ALU.mult).then_inc(made.sem, 1)

            def split(b, src, parts, ready, sig):
                pool.wait_ge(ready.sem, ready.at(b, 2))
                pool.tensor_tensor(rest[:], src[:], parts[:, 0, :], ALU.subtract).then_inc(sig.sem, 1)
                if sig is q_split:
                    add_bo(b)
                pool.tensor_tensor(parts[:, 1, :], src[:], parts[:, 0, :], ALU.subtract).then_inc(sig.sem, 1)
                pool.wait_ge(sig.sem, sig.at(b, 2))
                pool.tensor_tensor(parts[:, 2, :], rest[:], parts[:, 1, :], ALU.subtract).then_inc(sig.sem, 1)

            def split_max(b, g):
                pool.wait_ge(taken["max_rows"].sem, taken["max_rows"].at(b, 2 * (g + 1)))
                pool.tensor_tensor(max_rest[:], max_sb[:], max_parts[:, 0, :], ALU.subtract).then_inc(m_split.sem, 1)
                pool.tensor_tensor(max_parts[:, 1, :], max_sb[:], max_parts[:, 0, :], ALU.subtract).then_inc(m_split.sem, 1)
                if m_split.due(b, 3 * g + 2):
                    pool.wait_ge(m_split.sem, m_split.at(b, 3 * g + 2))
                pool.tensor_tensor(max_parts[:, 2, :], max_rest[:], max_parts[:, 1, :], ALU.subtract).then_inc(m_split.sem, 1)

            def add_bo(b):
                res = X[:, tokens(b, 0, C)].rearrange("p (c d) -> p c d", c=C)
                if isinstance(b, int) and b == 0:
                    pool.wait_ge(small_loaded, EARLY * 16)
                pool.tensor_tensor(res, res, bo_row[:].rearrange("p (a d) -> p a d", a=1).to_broadcast([P, C, D]),
                                   ALU.add).then_inc(bo_added.sem, 1)

            def gate_masks(b):
                pool.wait_ge(g_compared.sem, g_compared.at(b, 2))
                pool.tensor_tensor(g_ge[:], g_ge[:], earlier_b, ALU.mult).then_inc(g_masked.sem, 1)
                pool.tensor_tensor(x2_lo[:, tokens(b, 0, C)], x2_f[:], x2_hi[:, tokens(b, 0, C)].bitcast(F32),
                                   ALU.subtract).then_inc(x2_split.sem, 1)
                pool.tensor_tensor(g_gt[:], g_gt[:], later_b, ALU.mult).then_inc(g_masked.sem, 1)
                pool.wait_ge(g_masked.sem, g_masked.at(b, 2))
                pool.tensor_tensor(g_ge[:], g_ge[:], g_gt[:], ALU.add).then_inc(g_counted.sem, 1)

            earlier_b = earlier[:].rearrange("p (a e) f -> p a e f", a=1).to_broadcast([P, C, NE, NE])
            later_b = later[:].rearrange("p (a e) f -> p a e f", a=1).to_broadcast([P, C, NE, NE])

            def place(b, parity, u, half):
                if (u, half) == (3, 0) and exists(b + 2):
                    normalise(b + 2, mv, rstd, xn, mv_made, var_made, rstd_made, centred, xn_made, full["normed"])
                if (u, half) == (5, 0) and exists(b - 1):
                    normalise(b - 1, mv2, rstd2, xn2, mv2_made, var2_made, rstd2_made, centred2, xn2_made, full["normed2"])
                if (u, half) == (10, 1) and exists(b - 1):
                    gate_masks(b - 1)
                for name, bb, g in steps_at(b, u, half):
                    if name == "max_rows":
                        split_max(bb, g)
                    if name == "query":
                        pool.wait_ge(xn_made.sem, xn_made.at(bb, 1))
                        if k_split.due(bb - 1, 3):
                            pool.wait_ge(k_split.sem, k_split.at(bb - 1, 3))
                        split(bb, q_sb, q_parts, taken["query"], q_split)
                    if name == "key":
                        pool.wait_ge(q_split.sem, q_split.at(bb, 3))
                        split(bb, k_sb, k_parts, taken["key"], k_split)

            def slot(b, parity):
                for u in range(UNITS):
                    for half in range(2):
                        place(b, parity, u, half)
                    if isinstance(b, int) and b == NB - 1 and u >= UNITS - NE - 2:
                        e = u - (UNITS - NE - 2)
                        if e == 0:
                            pool.wait_ge(rows_filled, 6 * 16)
                        if e < 2:
                            load_w1(e)
                        elif e < NE:
                            pool.wait_ge(w1_split, e - 1)
                            load_w1(e)

            def load_w1(e):
                pool.dma_start(w_raw[:, e % 2, :], w1[e]).then_inc(w_loaded[e % 2], 16)

            def split_w2(e):
                pool.wait_ge(w2_hi_made, e + 1)
                pool.tensor_tensor(w2_lo[:, e], w2_raw[:, e], w2_hi[:, e].bitcast(F32), ALU.subtract).then_inc(w2_split, 1)

            run_slots(pool, slot)

            def add(t, e):
                pool.wait_ge(scaled_made.sem, scaled_made.at(t, e + 1))
                if e > 1:
                    if added.due(t, e - 1):
                        pool.wait_ge(added.sem, added.at(t, e - 1))
                if e == NE - 1:
                    if total_in_psum.due(t - 1, 1):
                        pool.wait_ge(total_in_psum.sem, total_in_psum.at(t - 1, 1))
                dst = total[:].rearrange("p c d -> p (c d)") if e == NE - 1 else acc[:]
                pool.tensor_tensor(dst, acc[:], scaled[:, e % 2, :], ALU.add).then_inc(added.sem, 1)

            def batch(t, before, now):
                if before:
                    add(t - 1, NE - 1)
                if isinstance(t, int) and t == 0:
                    split_w2(0)
                    split_w2(1)
                    for s in range(HU):
                        place(NB, 0, s // 2, s % 2)
                        if s % 4 == 1 and s // 4 + 2 < NE:
                            split_w2(s // 4 + 2)
                        if s % 4 == 3 and s >= 15:
                            add(t, s // 4 - 2)
                    add(t, NE - 2)
                elif now:
                    for e in range(1, NE - 1):
                        add(t, e)

            run_experts(pool, batch)

        @block.scalar
        def _(act):
            def exps(b, parity, u, js):
                for j in js:
                    n = GROUP * u + j
                    act.wait_ge(score_full.sem, score_full.at(b, n + 1))
                    if j == js[0]:
                        if u >= 2:
                            if pv_done.due(b, u - 1):
                                act.wait_ge(pv_done.sem, pv_done.at(b, u - 1))
                        else:
                            if pv_done.due(b - 1, UNITS - 1 + u):
                                act.wait_ge(pv_done.sem, pv_done.at(b - 1, UNITS - 1 + u))
                    nc.scalar.activation(probs[:, u % 2, j, :], psum[:, bank_of(SCORE, n, parity), :], ACT.Exp,
                                         scale=SCALE).then_inc(exp_done.sem, 1)

            def copy_pv(b, g):
                act.wait_ge(pv_done.sem, pv_done.at(b, 4 * (g + 1)))
                if full["heads"].due(b if g >= 2 else b - 1, g - 1 if g >= 2 else 3 + g):
                    act.wait_ge(full["heads"].sem, full["heads"].at(b if g >= 2 else b - 1, g - 1 if g >= 2 else 3 + g))
                nc.scalar.copy(pv_sb[:, g % 2, :], psum[:, PV, :]).then_inc(pv_copied.sem, 1)

            def take(name, b, parity, g):
                bank = psum[:, SHARED, :]

                def got():
                    act.wait_ge(full[name].sem, full[name].at(b, g + 1))

                if name == "max_rows":
                    got()
                    if m_split.due(b, 3 * g):
                        act.wait_ge(m_split.sem, m_split.at(b, 3 * g))
                    nc.scalar.copy(max_sb[:], bank[0:16, 0:P]).then_inc(taken[name].sem, 1)
                    if m_stored.due(b, 3 * g):
                        act.wait_ge(m_stored.sem, m_stored.at(b, 3 * g))
                    nc.scalar.copy(max_parts[:, 0, :], bank[0:16, 0:P]).then_inc(taken[name].sem, 1)
                elif name == "heads_t":
                    got()
                    if full["project"].due(b - 1, 1):
                        act.wait_ge(full["project"].sem, full["project"].at(b - 1, 1))
                    nc.scalar.copy(heads_t[:], bank).then_inc(taken[name].sem, 1)
                elif name == "normed":
                    got()
                    if full["latent"].due(b - 1, 1):
                        act.wait_ge(full["latent"].sem, full["latent"].at(b - 1, 1))
                    nc.scalar.copy(xn_hi[:], bank).then_inc(xn_hi_made.sem, 1)
                elif name == "normed2":
                    got()
                    if full["gate"].due(b - 1, 1):
                        act.wait_ge(full["gate"].sem, full["gate"].at(b - 1, 1))
                    if x2_split.due(b - 1, 1):
                        act.wait_ge(x2_split.sem, x2_split.at(b - 1, 1))
                    nc.scalar.copy(x2_f[:], bank).then_inc(taken[name].sem, 1)
                    nc.scalar.copy(x2_hi[:, tokens(b, 0, C)], bank).then_inc(taken[name].sem, 1)
                elif name == "query":
                    got()
                    if q_split.due(b - 1, 3):
                        act.wait_ge(q_split.sem, q_split.at(b - 1, 3))
                    nc.scalar.activation(q_sb[:], bank, ACT.Identity, bias=bq_sb[:, 0:1]).then_inc(taken[name].sem, 1)
                    if q_stored.due(b - 1, 6):
                        act.wait_ge(q_stored.sem, q_stored.at(b - 1, 6))
                    nc.scalar.activation(q_parts[:, 0, :], bank, ACT.Identity, bias=bq_sb[:, 0:1]).then_inc(taken[name].sem, 1)
                elif name == "key":
                    got()
                    if k_split.due(b - 1, 3):
                        act.wait_ge(k_split.sem, k_split.at(b - 1, 3))
                    nc.scalar.activation(k_sb[:], bank, ACT.Identity, bias=bk_sb[:, 0:1]).then_inc(taken[name].sem, 1)
                    if k_stored.due(b - 1, 6):
                        act.wait_ge(k_stored.sem, k_stored.at(b - 1, 6))
                    nc.scalar.activation(k_parts[:, 0, :], bank, ACT.Identity, bias=bk_sb[:, 0:1]).then_inc(taken[name].sem, 1)
                elif name == "latent":
                    got()
                    if full["value"].due(b - 1, 1):
                        act.wait_ge(full["value"].sem, full["value"].at(b - 1, 1))
                    nc.scalar.activation(lat_t[:], bank[0:LAT, :], ACT.Identity, bias=bl_sb[:, 0:1]).then_inc(taken[name].sem, 1)
                elif name == "gate_t":
                    got()
                    if cw_stored.due(b - 1, 1):
                        act.wait_ge(cw_stored.sem, cw_stored.at(b - 1, 1))
                    nc.scalar.copy(cw_t[:], bank[0:NE, :]).then_inc(taken[name].sem, 1)

            act.wait_ge(small_loaded, EARLY * 16)

            def place(b, parity, u, half):
                if half == 1 and u % 4 == 0:
                    bb, g = (b, u // 4 - 1) if u else (b - 1, 3)
                    if exists(bb):
                        copy_pv(bb, g)
                for name, bb, g in steps_at(b, u, half):
                    take(name, bb, parity, g)
                if (u, half) == (8, 0) and exists(b - 1):
                    act.wait_ge(taken["gate"].sem, taken["gate"].at(b - 1, 1))
                    nc.scalar.activation(g_e[:], g_z[:], ACT.Exp).then_inc(g_exp_done.sem, 1)

            def split_w2(e):
                nc.scalar.copy(w2_hi[:, e], w2_raw[:, e]).then_inc(w2_hi_made, 1)

            def slot(b, parity):
                for u in range(UNITS):
                    for half in range(2):
                        place(b, parity, u, half)
                        if exists(b):
                            exps(b, parity, u, (2 * half, 2 * half + 1))

            run_slots(act, slot)
            act.wait_ge(w2_loaded, 16)
            act.wait_ge(late_loaded, LATE * 16)
            split_w2(0)
            split_w2(1)

            def batch(t, before, now):
                for n in range(HU if now else 0):
                    if isinstance(t, int) and t == 0:
                        place(NB, 0, n // 2, n % 2)
                        if n % 4 == 1 and n // 4 + 2 < NE:
                            split_w2(n // 4 + 2)
                    act.wait_ge(hidden_full.sem, hidden_full.at(t, n + 1))
                    if n >= 4:
                        if h_lo_made.due(t, n - 3):
                            act.wait_ge(h_lo_made.sem, h_lo_made.at(t, n - 3))
                    else:
                        if h_lo_made.due(t - 1, HU - 3 + n):
                            act.wait_ge(h_lo_made.sem, h_lo_made.at(t - 1, HU - 3 + n))
                    nc.scalar.activation(h_sb[:, n % 4, :], psum[:, HIDDEN[n % 4], :], ACT.Gelu,
                                         bias=b1_sb[:, n:n + 1]).then_inc(gelu_done.sem, 1)

            run_experts(act, batch)

        @block.vector
        def _(dve):
            def set_ones():
                for i in range(2):
                    nc.vector.memset(values[:, i].rearrange("p c h k -> p (c h k)"), 1.0).then_inc(ones_made, 1)
                dve.wait_ge(ones_made, 2)
                dve.wait_ge(small_loaded, EARLY * 16)

            def split_projections():
                dve.wait_ge(small_loaded, EARLY * 16)
                for i, (w, hi, lo) in enumerate(((wq_sb, wq_hi, wq_lo), (wl_sb, wl_hi, wl_lo))):
                    nc.vector.tensor_copy(hi[:], w[:]).then_inc(proj_hi_made, 1)
                    dve.wait_ge(proj_hi_made, i + 1)
                    nc.vector.tensor_tensor(lo[:], w[:], hi[:].bitcast(F32), ALU.subtract).then_inc(proj_split, 1)

            def split_w1(e):
                dve.wait_ge(w_loaded[e % 2], 16 * (e // 2 + 1))
                nc.vector.tensor_copy(w1_hi[:, e, :], w_raw[:, e % 2, :]).then_inc(w1_hi_made, 1)
                dve.wait_ge(w1_hi_made, e + 1)
                nc.vector.tensor_tensor(w1_lo[:, e, :], w_raw[:, e % 2, :], w1_hi[:, e, :].bitcast(F32),
                                        ALU.subtract).then_inc(w1_split, 1)

            def ln_stats(b, stats_, made):
                for c in range(C):
                    nc.vector.bn_stats(stats_[:, c, :], X[:, tokens(b, c)]).then_inc(made.sem, 1)
                dve.wait_ge(made.sem, made.at(b, C))

            def ln_aggregate(b, stats_, mv_, mvm):
                for c in range(C):
                    nc.vector.bn_aggr(mv_[:, c, :], stats_[:, c, :]).then_inc(mvm.sem, 1)

            def take(name, b, parity, g):
                bank = psum[:, SHARED, :]
                if name == "heads":
                    view = bank.rearrange("p (c j k) -> p c j k", c=C, j=GROUP)
                    dve.wait_ge(full[name].sem, full[name].at(b, g + 1))
                    nc.vector.reciprocal(inv_sum[:], view[:, :, :, DH]).then_inc(inv_made.sem, 1)
                    dve.wait_ge(inv_made.sem, inv_made.at(b, g + 1))
                    if g == 0:
                        if full["heads_t"].due(b - 1, 1):
                            dve.wait_ge(full["heads_t"].sem, full["heads_t"].at(b - 1, 1))
                    nc.vector.tensor_tensor(heads[:, :, GROUP * g:GROUP * (g + 1), :], view[:, :, :, 0:DH],
                                            inv_sum[:].rearrange("p c (j a) -> p c j a", a=1).to_broadcast([P, C, GROUP, DH]),
                                            ALU.mult).then_inc(taken[name].sem, 1)
                elif name == "normed":
                    dve.wait_ge(full[name].sem, full[name].at(b, 1))
                    dve.wait_ge(xn_hi_made.sem, xn_hi_made.at(b, 1))
                    nc.vector.tensor_tensor(xn_lo[:], bank, xn_hi[:].bitcast(F32), ALU.subtract).then_inc(taken[name].sem, 1)
                elif name == "value":
                    dve.wait_ge(full[name].sem, full[name].at(b, 1))
                    nc.vector.tensor_tensor(values[:, parity_of(b, parity), :, :, 0:DH],
                                            bank.rearrange("p (c h d) -> p c h d", c=C, h=H),
                                            bv_row[:].rearrange("p (a h d) -> p a h d", a=1, h=H).to_broadcast([P, C, H, DH]),
                                            ALU.add).then_inc(taken[name].sem, 1)
                elif name == "project":
                    dve.wait_ge(full[name].sem, full[name].at(b, 1))
                    dve.wait_ge(bo_added.sem, bo_added.at(b, 1))
                    nc.vector.tensor_tensor(X[:, tokens(b, 0, C)], bank, X[:, tokens(b, 0, C)], ALU.add).then_inc(taken[name].sem, 1)
                    dve.wait_ge(taken[name].sem, taken[name].at(b, 1))
                elif name == "gate":
                    logits = bank[:, 0:C * NE].rearrange("p (c e) -> p c e", c=C)
                    dve.wait_ge(full[name].sem, full[name].at(b, 1))
                    nc.vector.tensor_reduce(g_max[:], logits, AX_X, ALU.max).then_inc(g_max_made.sem, 1)
                    dve.wait_ge(g_max_made.sem, g_max_made.at(b, 1))
                    nc.vector.tensor_tensor(g_z[:], logits, g_max[:].rearrange("p (c a) -> p c a", a=1).to_broadcast([P, C, NE]),
                                            ALU.subtract).then_inc(taken[name].sem, 1)

            def parity_of(b, parity):
                return 1 - parity

            def gate_softmax(b):
                dve.wait_ge(g_exp_done.sem, g_exp_done.at(b, 1))
                nc.vector.tensor_reduce(g_sum[:], g_e[:], AX_X, ALU.add).then_inc(g_sum_made.sem, 1)
                dve.wait_ge(g_sum_made.sem, g_sum_made.at(b, 1))
                nc.vector.reciprocal(g_inv[:], g_sum[:]).then_inc(g_inv_made.sem, 1)
                dve.wait_ge(g_inv_made.sem, g_inv_made.at(b, 1))
                nc.vector.tensor_tensor(g_p[:], g_e[:], g_inv[:].rearrange("p (c a) -> p c a", a=1).to_broadcast([P, C, NE]),
                                        ALU.mult).then_inc(g_p_made.sem, 1)
                dve.wait_ge(g_p_made.sem, g_p_made.at(b, 1))
                own = g_p[:].rearrange("p c (e a) -> p c e a", a=1).to_broadcast([P, C, NE, NE])
                other = g_p[:].rearrange("p c (a f) -> p c a f", a=1).to_broadcast([P, C, NE, NE])
                nc.vector.tensor_tensor(g_ge[:], other, own, ALU.is_ge).then_inc(g_compared.sem, 1)
                nc.vector.tensor_tensor(g_gt[:], other, own, ALU.is_gt).then_inc(g_compared.sem, 1)

            def gate_choice(b):
                dve.wait_ge(g_counted.sem, g_counted.at(b, 1))
                nc.vector.tensor_reduce(g_rank[:], g_ge[:], AX_X, ALU.add).then_inc(g_ranked.sem, 1)
                dve.wait_ge(g_ranked.sem, g_ranked.at(b, 1))
                if full["gate_t"].due(b - 1, 1):
                    dve.wait_ge(full["gate_t"].sem, full["gate_t"].at(b - 1, 1))
                nc.vector.scalar_tensor_tensor(out=cw[:], in0=g_rank[:], scalar=1.5, in1=g_p[:], op0=ALU.is_lt,
                                               op1=ALU.mult).then_inc(cw_made.sem, 1)

            def maxima(b, parity, v, i0):
                g = v // 4
                for i in (i0, i0 + 1):
                    n = GROUP * v + i
                    dve.wait_ge(max_full.sem, max_full.at(b, n + 1))
                    if v % 4 == 0 and i == 0:
                        if g >= 2:
                            if full["max_rows"].due(b, g - 1):
                                dve.wait_ge(full["max_rows"].sem, full["max_rows"].at(b, g - 1))
                        else:
                            if full["max_rows"].due(b - 1, 3 + g):
                                dve.wait_ge(full["max_rows"].sem, full["max_rows"].at(b - 1, 3 + g))
                    nc.vector.tensor_reduce(neg_max[:, g % 2, 4 * (v % 4) + i:4 * (v % 4) + i + 1],
                                            psum[:, bank_of(MAXIMA, n, parity), :], AX_X, ALU.max,
                                            negate=True).then_inc(max_read.sem, 1)

            nc.vector.memset(w_raw[:, 0, :], 0.0).then_inc(fill_made, 1)
            nc.vector.memset(w_raw[:, 1, :].bitcast(mybir.dt.uint32), TWO_ONES).then_inc(fill_made, 1)

            def place(b, parity, u, half):
                if (u, half) == (1, 0) and exists(b + 2):
                    if xn_made.due(b + 1, 1):
                        dve.wait_ge(xn_made.sem, xn_made.at(b + 1, 1))
                if (u, half) == (3, 1) and exists(b - 1):
                    if xn2_made.due(b - 2, 1):
                        dve.wait_ge(xn2_made.sem, xn2_made.at(b - 2, 1))
                if (u, half) == (3, 0) and isinstance(b, int) and b == -2:
                    split_projections()
                if (u, half) == (1, 1) and exists(b + 2):
                    wait_x(dve, b + 2)
                    ln_stats(b + 2, stats, stats_made)
                if (u, half) == (2, 1) and exists(b + 2):
                    ln_aggregate(b + 2, stats, mv, mv_made)
                if (u, half) == (4, 0) and exists(b - 1):
                    ln_stats(b - 1, stats2, stats2_made)
                if (u, half) == (4, 1) and exists(b - 1):
                    ln_aggregate(b - 1, stats2, mv2, mv2_made)
                for name, bb, g in steps_at(b, u, half):
                    take(name, bb, parity, g)
                if (u, half) == (8, 0) and exists(b - 1):
                    gate_softmax(b - 1)
                if (u, half) == (12, 0) and exists(b - 1):
                    gate_choice(b - 1)

            def slot(b, parity):
                for u in range(UNITS):
                    for half in range(2):
                        place(b, parity, u, half)
                        bb, v = maxima_at(b, u)
                        if exists(bb):
                            maxima(bb, parity if u < UNITS - AHEAD else 1 - parity, v, 2 * half)
                        if isinstance(b, int) and b == NB - 1 and u >= UNITS - NE and half == 0:
                            if u == UNITS - NE:
                                dve.wait_ge(score_full.sem, score_full.at(NB - 2, NT))
                            split_w1(u - (UNITS - NE))

            run_slots(dve, slot, set_ones)
            dve.wait_ge(pv_done.sem, pv_done.at(NB - 1, UNITS))
            dve.wait_ge(late_loaded, LATE * 16)

            def scale(t, e):
                dve.wait_ge(second_done.sem, second_done.at(t, HC * (e + 1)))
                dve.wait_ge(cw_loaded[e].sem, cw_loaded[e].at(t, 1))
                if e == 0:
                    if added.due(t - 1, NE - 1):
                        dve.wait_ge(added.sem, added.at(t - 1, NE - 1))
                elif e >= 3:
                    if added.due(t, e - 2):
                        dve.wait_ge(added.sem, added.at(t, e - 2))
                dst = acc[:] if e == 0 else scaled[:, e % 2, :]
                nc.vector.scalar_tensor_tensor(out=dst, in0=psum[:, EXPERT_OUT[e % 2], :], scalar=b2_sb[:, e:e + 1],
                                               in1=cw_row[:, e, :], op0=ALU.add, op1=ALU.mult).then_inc(scaled_made.sem, 1)

            def finish(t):
                dve.wait_ge(total_in_psum.sem, total_in_psum.at(t, 1))
                if result_stored.due(t - 1, 1):
                    dve.wait_ge(result_stored.sem, result_stored.at(t - 1, 1))
                nc.vector.tensor_tensor(result[:].rearrange("p c d -> p (c d)"), psum[:, SHARED, :], X[:, tokens(t, 0, C)],
                                        ALU.add).then_inc(result_made.sem, 1)

            def batch(t, before, now):
                for n in range(HU if now else 8):
                    if isinstance(t, int) and t == 0:
                        place(NB, 0, n // 2, n % 2)
                    if now:
                        dve.wait_ge(gelu_done.sem, gelu_done.at(t, n + 1))
                        if n >= 4:
                            if second_done.due(t, n - 3):
                                dve.wait_ge(second_done.sem, second_done.at(t, n - 3))
                        else:
                            if second_done.due(t - 1, HU - 3 + n):
                                dve.wait_ge(second_done.sem, second_done.at(t - 1, HU - 3 + n))
                        nc.vector.tensor_copy(h_hi[:, n % 4, :], h_sb[:, n % 4, :]).then_inc(h_hi_made.sem, 1)
                        dve.wait_ge(h_hi_made.sem, h_hi_made.at(t, n + 1))
                        nc.vector.tensor_tensor(h_lo[:, n % 4, :], h_sb[:, n % 4, :], h_hi[:, n % 4, :].bitcast(F32),
                                                ALU.subtract).then_inc(h_lo_made.sem, 1)
                    if n == 2 and before:
                        scale(t - 1, NE - 1)
                    if n == 7 and before:
                        finish(t - 1)
                    if now and n >= 6 and (n - 6) % 4 == 0:
                        scale(t, (n - 6) // 4)

            run_experts(dve, batch)

        @block.tensor
        def _(pe):
            def shared_bank_free(b, index):
                for name, bb, g in reversed(order_before(b, index)):
                    pe.wait_ge(taken[name].sem, taken[name].at(bb, READS.get(name, 1) * (g + 1)))
                    return

            def order_before(b, index):
                found = [(n, b - 1 + db, g) for _, _, n, db, g in STEPS if exists(b - 1 + db)]
                return found + [(n, b + db, g) for _, _, n, db, g in STEPS[:index] if exists(b + db)]

            def step(name, b, parity, g):
                bank = psum[:, SHARED, :]

                def transposes(src, n, rows):
                    for c in range(n):
                        mm = pe.transpose(bank[:, c * P:(c + 1) * P], src(c), ident[:])
                    return mm

                def three_passes(out_, w_hi, w_lo):
                    pe.matmul(out_, w_hi, xn_hi[:], start=True, stop=False)
                    pe.matmul(out_, w_hi, xn_lo[:], start=False, stop=False)
                    return pe.matmul(out_, w_lo, xn_hi[:], start=False, stop=True)

                if name == "max_rows":
                    pe.wait_ge(max_read.sem, max_read.at(b, 16 * (g + 1)))
                    mm = pe.transpose(bank[0:16, 0:P], neg_max[:, g % 2, :], ident[:])
                elif name == "heads":
                    pe.wait_ge(pv_copied.sem, pv_copied.at(b, g + 1))
                    mm = transposes(lambda c: pv_sb[:, g % 2, c * P:(c + 1) * P], C, P)
                elif name == "heads_t":
                    pe.wait_ge(taken["heads"].sem, taken["heads"].at(b, GROUP))
                    mm = transposes(lambda c: heads[:, c].rearrange("p h d -> p (h d)"), C, P)
                elif name == "project":
                    pe.wait_ge(taken["heads_t"].sem, taken["heads_t"].at(b, 1))
                    for c in range(C):
                        mm = pe.matmul(bank[:, c * P:(c + 1) * P], heads_t[:, c * P:(c + 1) * P], wo_sb[:], start=True, stop=True)
                elif name == "normed":
                    pe.wait_ge(xn_made.sem, xn_made.at(b, 1))
                    mm = transposes(lambda c: xn[:, c], C, P)
                elif name == "normed2":
                    pe.wait_ge(xn2_made.sem, xn2_made.at(b, 1))
                    mm = transposes(lambda c: xn2[:, c], C, P)
                elif name == "query":
                    pe.wait_ge(taken["normed"].sem, taken["normed"].at(b, 1))
                    if isinstance(b, int) and b == 0:
                        pe.wait_ge(proj_split, 2)
                    mm = three_passes(bank, wq_hi[:], wq_lo[:])
                elif name == "latent":
                    mm = three_passes(bank[0:LAT, :], wl_hi[:], wl_lo[:])
                elif name == "key":
                    pe.wait_ge(taken["latent"].sem, taken["latent"].at(b, 1))
                    mm = pe.matmul(bank, wk_sb[:], lat_t[:], start=True, stop=True)
                elif name == "value":
                    for c in range(C):
                        mm = pe.matmul(bank[:, c * P:(c + 1) * P], lat_t[:, c * P:(c + 1) * P], wv_sb[:], start=True, stop=True)
                elif name == "gate":
                    pe.wait_ge(taken["normed2"].sem, taken["normed2"].at(b, 2))
                    for c in range(C):
                        mm = pe.matmul(bank[:, c * NE:(c + 1) * NE], x2_f[:, c * P:(c + 1) * P], wg_sb[:], start=True, stop=True)
                elif name == "gate_t":
                    pe.wait_ge(cw_made.sem, cw_made.at(b, 1))
                    for c in range(C):
                        mm = pe.transpose(bank[0:NE, c * P:(c + 1) * P], cw[:, c], ident[:])
                mm.then_inc(full[name].sem, 1)

            def scores(b, parity, u, js):
                g, kc = u // 4, u % 4
                for j in js:
                    n, h = GROUP * u + j, GROUP * g + j
                    bb, k = bank_freed(SCORE, n, b, parity)
                    if exp_done.due(bb, k):
                        pe.wait_ge(exp_done.sem, exp_done.at(bb, k))
                    if kc == 0 and j == 0:
                        pe.wait_ge(stacked[g].sem, stacked[g].at(b, 2))
                        pe.wait_ge(m_stored.sem, m_stored.at(b, 3 * (g + 1)))
                    pe.matmul(psum[:, bank_of(SCORE, n, parity), :],
                              K_stack[parity][0:MAX_ROW + 3, h, kc * P:(kc + 1) * P],
                              Q_stack[parity][0:MAX_ROW + 3, h, :], start=True, stop=True).then_inc(score_full.sem, 1)

            def score_rows(b, parity, v, chunks):
                for i in chunks:
                    n = GROUP * v + i
                    bb, k = bank_freed(MAXIMA, n, b, parity)
                    if max_read.due(bb, k):
                        pe.wait_ge(max_read.sem, max_read.at(bb, k))
                    if v % 4 == 0 and i == 0:
                        pe.wait_ge(stacked[v // 4].sem, stacked[v // 4].at(b, 2))
                    pe.matmul(psum[:, bank_of(MAXIMA, n, parity), :],
                              Q_stack[parity][0:MAX_ROW, v, i * P:(i + 1) * P],
                              K_stack[parity][0:MAX_ROW, v, :], start=True, stop=True).then_inc(max_full.sem, 1)

            def weighted(b, parity, u):
                g, kc = u // 4, u % 4
                pe.wait_ge(exp_done.sem, exp_done.at(b, GROUP * (u + 1)))
                if u == 0:
                    pe.wait_ge(taken["value"].sem, taken["value"].at(b, 1))
                if kc == 0:
                    bb, k = (b, g) if g else (b - 1, GROUP)
                    if pv_copied.due(bb, k):
                        pe.wait_ge(pv_copied.sem, pv_copied.at(bb, k))
                for j in range(GROUP):
                    mm = pe.matmul(psum[32 * j:32 * (j + 1), PV, :], values[:, parity, kc, GROUP * g + j, :],
                                   probs[:, u % 2, j, :], start=(kc == 0), stop=(kc == C - 1))
                mm.then_inc(pv_done.sem, 1)

            pe.wait_ge(consts_made, 8)
            pe.wait_ge(small_loaded, EARLY * 16)

            def place(b, parity, u, half):
                for index, (v, w, name, db, g) in enumerate(STEPS):
                    if (v, w) == (u, half) and exists(b + db):
                        shared_bank_free(b, index)
                        step(name, b + db, parity, g)

            def slot(b, parity):
                for u in range(UNITS):
                    for half in range(2):
                        place(b, parity, u, half)
                        bb, v = maxima_at(b, u)
                        for j in (2 * half, 2 * half + 1):
                            if exists(b):
                                scores(b, parity, u, (j,))
                            if exists(bb):
                                score_rows(bb, parity if u < UNITS - AHEAD else 1 - parity, v, (j,))
                        if half == 0:
                            if u and exists(b):
                                weighted(b, parity, u - 1)
                            if not u and exists(b - 1):
                                weighted(b - 1, 1 - parity, UNITS - 1)

            def after_first():
                pe.wait_ge(late_loaded, LATE * 16)
                pe.wait_ge(ones_made, 2)
                pe.wait_ge(rows_filled, 6 * 16)

            run_slots(pe, slot, after_first)
            pe.wait_ge(exp_done.sem, exp_done.at(NB - 1, NT))
            pe.wait_ge(max_read.sem, max_read.at(NB - 1, NT))
            weighted(NB - 1, (NB - 1) % 2, UNITS - 1)

            def first(t, n):
                e, c = n // HC, n % HC
                if n >= 4:
                    if gelu_done.due(t, n - 3):
                        pe.wait_ge(gelu_done.sem, gelu_done.at(t, n - 3))
                else:
                    if gelu_done.due(t - 1, HU - 3 + n):
                        pe.wait_ge(gelu_done.sem, gelu_done.at(t - 1, HU - 3 + n))
                if isinstance(t, int) and t == 0 and c == 0:
                    pe.wait_ge(w1_split, e + 1)
                if n == 0 and isinstance(t, int):
                    pe.wait_ge(x2_split.sem, x2_split.at(NB - 1 if t == NB - 1 else NB - 2, 1))
                cols = slice(c * P, (c + 1) * P)
                bank = psum[:, HIDDEN[n % 4], :]
                pe.matmul(bank, w1_hi[:, e, cols], x2_hi[:, tokens(t, 0, C)], start=True, stop=False)
                pe.matmul(bank, w1_hi[:, e, cols], x2_lo[:, tokens(t, 0, C)], start=False, stop=False)
                pe.matmul(bank, w1_lo[:, e, cols], x2_hi[:, tokens(t, 0, C)], start=False, stop=True).then_inc(hidden_full.sem, 1)

            def second(t, n):
                e, c = n // HC, n % HC
                pe.wait_ge(h_lo_made.sem, h_lo_made.at(t, n + 1))
                if isinstance(t, int) and t == 0 and c == 0:
                    pe.wait_ge(w2_split, e + 1)
                if c == 0:
                    if e >= 2:
                        if scaled_made.due(t, e - 1):
                            pe.wait_ge(scaled_made.sem, scaled_made.at(t, e - 1))
                    else:
                        if scaled_made.due(t - 1, NE - 1 + e):
                            pe.wait_ge(scaled_made.sem, scaled_made.at(t - 1, NE - 1 + e))
                bank = psum[:, EXPERT_OUT[e % 2], :]
                pe.matmul(bank, w2_hi[:, e, c, :], h_hi[:, n % 4, :], start=(c == 0), stop=False)
                pe.matmul(bank, w2_hi[:, e, c, :], h_lo[:, n % 4, :], start=False, stop=False)
                pe.matmul(bank, w2_lo[:, e, c, :], h_hi[:, n % 4, :], start=False, stop=(c == HC - 1)).then_inc(second_done.sem, 1)

            def batch(t, before, now):
                for n in range(HU if now else 8):
                    if isinstance(t, int) and t == 0:
                        place(NB, 0, n // 2, n % 2)
                    if now:
                        first(t, n)
                    if n < LAG:
                        if before:
                            second(t - 1, HU - LAG + n)
                    elif now:
                        second(t, n - LAG)
                    if n == 6 and before:
                        if added.due(t - 1, NE - 1):
                            pe.wait_ge(added.sem, added.at(t - 1, NE - 1))
                        if isinstance(t, int) and t == 1:
                            pe.wait_ge(taken["gate_t"].sem, taken["gate_t"].at(NB - 1, 1))
                        if result_made.due(t - 2, 1):
                            pe.wait_ge(result_made.sem, result_made.at(t - 2, 1))
                        for c in range(C):
                            mm = pe.transpose(psum[:, SHARED, c * P:(c + 1) * P], total[:, c], ident[:])
                        mm.then_inc(total_in_psum.sem, 1)

            run_experts(pe, batch)


def kernel(**inputs):
    import numpy as _np
    import concourse.bacc as _bacc
    from concourse import mybir as _mybir
    from concourse.bass_utils import run_bass_kernel_spmd as _run

    def arr(name):
        return _np.ascontiguousarray(inputs[name])

    x, b1 = arr("L0_attn_x"), arr("L0_ffn_b1")
    laid_out = {
        "x": x, "wq": arr("L0_attn_Wq"), "bq": arr("L0_attn_bq"), "wl": arr("L0_attn_Wl"), "bl": arr("L0_attn_bl"),
        "wk": arr("L0_attn_Wk"), "bk": arr("L0_attn_bk"), "wv": arr("L0_attn_Wv"), "bv": arr("L0_attn_bv"),
        "wo": arr("L0_attn_Wo"), "bo": arr("L0_attn_bo"),
        "w_gate_t": _np.ascontiguousarray(arr("L0_ffn_w_gate").T), "w1": arr("L0_ffn_W1"),
        "b1_t": _np.ascontiguousarray(b1.reshape(-1, 128).T), "w2": arr("L0_ffn_W2"),
        "b2_t": _np.ascontiguousarray(arr("L0_ffn_b2").T),
    }
    nc = _bacc.Bacc("TRN2", target_bir_lowering=False, num_devices=1)
    args = {n: nc.dram_tensor(f"in_{n}", a.shape, _mybir.dt.from_np(a.dtype), kind="ExternalInput").ap()
            for n, a in laid_out.items()}
    out = nc.dram_tensor("out_0", x.shape, _mybir.dt.from_np(x.dtype), kind="ExternalOutput").ap()
    block_attention_moe(nc, **args, out=out)
    r = _run(nc, [{f"in_{n}": a for n, a in laid_out.items()}], core_ids=[0])
    return r.results[0]["out_0"]
```
